# Optimizing a Trainium2 kernel written in Bass

```python
import numpy as np
import jax
import jax.numpy as jnp

def _softmax(x, axis=-1):
    return jax.nn.softmax(x, axis=axis)

def _gelu(x):
    return jax.nn.gelu(x, approximate=True)

def _silu(x):
    return jax.nn.silu(x)

def _sigmoid(x):
    return jax.nn.sigmoid(x)

def _layernorm(x, axis=-1, eps=1e-05):
    m = jnp.mean(x, axis=axis, keepdims=True)
    v = jnp.var(x, axis=axis, keepdims=True)
    return (x - m) / jnp.sqrt(v + eps)

def _scatter_add(tgt, idx, src, axis=0):
    return tgt.at[idx].add(src)

def _segment_sum(src, seg, n):
    return jax.ops.segment_sum(src, seg, n)
kernel_name = 'mk_seq_postln_d2_jaxref_r8_36e66a'

def setup_inputs(seed: int=0):
    np.random.seed(seed)
    _w = jnp.asarray

    def _L0_attn_setup():
        import jax, jax.numpy as jnp
        import numpy as np
        H = 512
        D = H // 4
        key = jax.random.key(seed)
        k1, k2, k3, k4, k5 = jax.random.split(key, 5)
        x = jax.random.normal(k1, (4, 512, H), dtype=jnp.float32)
        s_in = 1.0 / np.sqrt(H)
        Wqkv = jax.random.normal(k2, (H, 3 * D), dtype=jnp.float32) * s_in
        bqkv = jax.random.normal(k3, (3 * D,), dtype=jnp.float32) * 0.01
        Wo = jax.random.normal(k4, (D, H), dtype=jnp.float32) * (1.0 / np.sqrt(D))
        bo = jax.random.normal(k5, (H,), dtype=jnp.float32) * 0.01
        return {'x': x, 'Wqkv': Wqkv, 'bqkv': bqkv, 'Wo': Wo, 'bo': bo}
    _L0_attn_in = _L0_attn_setup()

    def _L0_ffn_setup():
        import jax, jax.numpy as jnp
        import numpy as np
        THRESH_FACTOR = 0.7

        def _bitlinear(x, w, scale):
            w_abs = jnp.abs(w)
            thr = jnp.mean(w_abs) * THRESH_FACTOR
            wq = jnp.sign(w) * (w_abs > thr).astype(w.dtype)
            w_scaled = wq * scale
            return jnp.einsum('bsd,od->bso', x, w_scaled)
        key = jax.random.key(seed)
        k1, k2, k3, k4 = jax.random.split(key, 4)
        dim, hidden = (512, 2048)
        x = jax.random.normal(k1, (2, 256, dim), dtype=jnp.float32)
        gate_w = jax.random.normal(k2, (hidden, dim), dtype=jnp.float32) / np.sqrt(dim)
        up_w = jax.random.normal(k3, (hidden, dim), dtype=jnp.float32) / np.sqrt(dim)
        down_w = jax.random.normal(k4, (dim, hidden), dtype=jnp.float32) / np.sqrt(hidden)
        return {'x': x, 'gate_w': gate_w, 'gate_scale': jnp.ones((hidden, 1), jnp.float32), 'up_w': up_w, 'up_scale': jnp.ones((hidden, 1), jnp.float32), 'down_w': down_w, 'down_scale': jnp.ones((dim, 1), jnp.float32)}
    _L0_ffn_in = _L0_ffn_setup()

    def _L1_attn_setup():
        import jax, jax.numpy as jnp
        import numpy as np
        H = 512
        D = H // 4
        key = jax.random.key(seed)
        k1, k2, k3, k4, k5 = jax.random.split(key, 5)
        x = jax.random.normal(k1, (4, 512, H), dtype=jnp.float32)
        s_in = 1.0 / np.sqrt(H)
        Wqkv = jax.random.normal(k2, (H, 3 * D), dtype=jnp.float32) * s_in
        bqkv = jax.random.normal(k3, (3 * D,), dtype=jnp.float32) * 0.01
        Wo = jax.random.normal(k4, (D, H), dtype=jnp.float32) * (1.0 / np.sqrt(D))
        bo = jax.random.normal(k5, (H,), dtype=jnp.float32) * 0.01
        return {'x': x, 'Wqkv': Wqkv, 'bqkv': bqkv, 'Wo': Wo, 'bo': bo}
    _L1_attn_in = _L1_attn_setup()

    def _L1_ffn_setup():
        import jax, jax.numpy as jnp
        import numpy as np
        NF4_CODE = jnp.array([-1.0, -0.6961928009986877, -0.5250730514526367, -0.39491748809814453, -0.28444138169288635, -0.18477343022823334, -0.09105003625154495, 0.0, 0.07958029955625534, 0.16093020141124725, 0.24611230194568634, 0.33791524171829224, 0.44070982933044434, 0.5626170039176941, 0.7229568362236023, 1.0], dtype=jnp.float32)
        BLOCKSIZE = 64

        def nf4_quant_dequant(w):
            shape = w.shape
            flat = w.reshape(-1, BLOCKSIZE)
            absmax = jnp.max(jnp.abs(flat), axis=1, keepdims=True)
            normalized = flat / jnp.where(absmax == 0, 1.0, absmax)
            bounds = (NF4_CODE[:-1] + NF4_CODE[1:]) * 0.5
            idx = jnp.searchsorted(bounds, normalized)
            return (NF4_CODE[idx] * absmax).reshape(shape)
        key = jax.random.key(seed)
        k1, k2, k3, kx = jax.random.split(key, 4)
        D, H = (512, 1376)
        scale = 0.02
        w1 = jax.random.normal(k1, (H, D), jnp.float32) * scale
        w2 = jax.random.normal(k2, (H, D), jnp.float32) * scale
        w3 = jax.random.normal(k3, (D, H), jnp.float32) * scale
        x = jax.random.normal(kx, (2, 256, D), jnp.float32)
        return {'x': x, 'w1': w1, 'w2': w2, 'w3': w3}
    _L1_ffn_in = _L1_ffn_setup()
    _d = {'L0_attn_x': _L0_attn_in['x'], 'L0_attn_Wqkv': _L0_attn_in['Wqkv'], 'L0_attn_bqkv': _L0_attn_in['bqkv'], 'L0_attn_Wo': _L0_attn_in['Wo'], 'L0_attn_bo': _L0_attn_in['bo'], 'L0_ffn_gate_w': _L0_ffn_in['gate_w'], 'L0_ffn_gate_scale': _L0_ffn_in['gate_scale'], 'L0_ffn_up_w': _L0_ffn_in['up_w'], 'L0_ffn_up_scale': _L0_ffn_in['up_scale'], 'L0_ffn_down_w': _L0_ffn_in['down_w'], 'L0_ffn_down_scale': _L0_ffn_in['down_scale'], 'L1_attn_Wqkv': _L1_attn_in['Wqkv'], 'L1_attn_bqkv': _L1_attn_in['bqkv'], 'L1_attn_Wo': _L1_attn_in['Wo'], 'L1_attn_bo': _L1_attn_in['bo'], 'L1_ffn_w1': _L1_ffn_in['w1'], 'L1_ffn_w2': _L1_ffn_in['w2'], 'L1_ffn_w3': _L1_ffn_in['w3']}
    _x0 = _d['L0_attn_x']
    _d['L0_attn_x'] = jax.random.normal(jax.random.fold_in(jax.random.key(seed), 1), (4, 512, 512), dtype=_x0.dtype)
    del _x0
    return _d

def reference(L0_attn_x, L0_attn_Wqkv, L0_attn_bqkv, L0_attn_Wo, L0_attn_bo, L0_ffn_gate_w, L0_ffn_gate_scale, L0_ffn_up_w, L0_ffn_up_scale, L0_ffn_down_w, L0_ffn_down_scale, L1_attn_Wqkv, L1_attn_bqkv, L1_attn_Wo, L1_attn_bo, L1_ffn_w1, L1_ffn_w2, L1_ffn_w3):

    def _L0_attn_ref(x, Wqkv, bqkv, Wo, bo):
        import jax, jax.numpy as jnp
        import numpy as np
        H = 512
        D = H // 4
        B, S, C = x.shape
        d = C // 4
        qkv = jnp.einsum('bsc,cf->bsf', x, Wqkv) + bqkv
        qkv = qkv.reshape(B, S, 3, d)
        q, k, v = (qkv[:, :, 0], qkv[:, :, 1], qkv[:, :, 2])
        scale = 1.0 / jnp.sqrt(jnp.float32(d)).astype(x.dtype)
        attn = jnp.einsum('bqd,bkd->bqk', q, k) * scale
        attn = jax.nn.softmax(attn, axis=-1)
        out = jnp.einsum('bqk,bkd->bqd', attn, v)
        return jnp.einsum('bqd,dc->bqc', out, Wo) + bo

    def _L0_ffn_ref(x, gate_w, gate_scale, up_w, up_scale, down_w, down_scale):
        import jax, jax.numpy as jnp
        import numpy as np
        THRESH_FACTOR = 0.7

        def _bitlinear(x, w, scale):
            w_abs = jnp.abs(w)
            thr = jnp.mean(w_abs) * THRESH_FACTOR
            wq = jnp.sign(w) * (w_abs > thr).astype(w.dtype)
            w_scaled = wq * scale
            return jnp.einsum('bsd,od->bso', x, w_scaled)
        gate = _bitlinear(x, gate_w, gate_scale)
        up = _bitlinear(x, up_w, up_scale)
        hidden = jax.nn.silu(gate) * up
        out = _bitlinear(hidden, down_w, down_scale)
        return out

    def _L1_attn_ref(x, Wqkv, bqkv, Wo, bo):
        import jax, jax.numpy as jnp
        import numpy as np
        H = 512
        D = H // 4
        B, S, C = x.shape
        d = C // 4
        qkv = jnp.einsum('bsc,cf->bsf', x, Wqkv) + bqkv
        qkv = qkv.reshape(B, S, 3, d)
        q, k, v = (qkv[:, :, 0], qkv[:, :, 1], qkv[:, :, 2])
        scale = 1.0 / jnp.sqrt(jnp.float32(d)).astype(x.dtype)
        attn = jnp.einsum('bqd,bkd->bqk', q, k) * scale
        attn = jax.nn.softmax(attn, axis=-1)
        out = jnp.einsum('bqk,bkd->bqd', attn, v)
        return jnp.einsum('bqd,dc->bqc', out, Wo) + bo

    def _L1_ffn_ref(x, w1, w2, w3):
        import jax, jax.numpy as jnp
        import numpy as np
        NF4_CODE = jnp.array([-1.0, -0.6961928009986877, -0.5250730514526367, -0.39491748809814453, -0.28444138169288635, -0.18477343022823334, -0.09105003625154495, 0.0, 0.07958029955625534, 0.16093020141124725, 0.24611230194568634, 0.33791524171829224, 0.44070982933044434, 0.5626170039176941, 0.7229568362236023, 1.0], dtype=jnp.float32)
        BLOCKSIZE = 64

        def nf4_quant_dequant(w):
            shape = w.shape
            flat = w.reshape(-1, BLOCKSIZE)
            absmax = jnp.max(jnp.abs(flat), axis=1, keepdims=True)
            normalized = flat / jnp.where(absmax == 0, 1.0, absmax)
            bounds = (NF4_CODE[:-1] + NF4_CODE[1:]) * 0.5
            idx = jnp.searchsorted(bounds, normalized)
            return (NF4_CODE[idx] * absmax).reshape(shape)
        dq1 = nf4_quant_dequant(w1)
        dq2 = nf4_quant_dequant(w2)
        dq3 = nf4_quant_dequant(w3)
        gate = jnp.einsum('bsd,hd->bsh', x, dq1)
        up = jnp.einsum('bsd,hd->bsh', x, dq2)
        h = jax.nn.silu(gate) * up
        return jnp.einsum('bsh,dh->bsd', h, dq3)
    x = L0_attn_x
    x = _layernorm(x + _L0_attn_ref(x, L0_attn_Wqkv, L0_attn_bqkv, L0_attn_Wo, L0_attn_bo), axis=-1)
    x = _layernorm(x + _L0_ffn_ref(x, L0_ffn_gate_w, L0_ffn_gate_scale, L0_ffn_up_w, L0_ffn_up_scale, L0_ffn_down_w, L0_ffn_down_scale), axis=-1)
    x = _layernorm(x + _L1_attn_ref(x, L1_attn_Wqkv, L1_attn_bqkv, L1_attn_Wo, L1_attn_bo), axis=-1)
    x = _layernorm(x + _L1_ffn_ref(x, L1_ffn_w1, L1_ffn_w2, L1_ffn_w3), axis=-1)
    return x

_drawn_inputs = setup_inputs


def setup_inputs(seed=0):
    import zlib

    import numpy as np

    out = dict(_drawn_inputs(seed))
    spreads = {'L0_ffn_gate_scale': (1.0, 0.2),
     'L0_ffn_up_scale': (1.0, 0.2),
     'L0_ffn_down_scale': (1.0, 0.2)}
    factors = {'L0_attn_bqkv': 3.597, 'L0_attn_bo': 3.903, 'L1_attn_bqkv': 5.176, 'L1_attn_bo': 5.79}
    for name, (base, spread) in spreads.items():
        noise = np.random.default_rng([zlib.crc32(name.encode()), seed]).standard_normal(out[name].shape)
        drawn = base * np.exp(spread * noise) if base else spread * noise
        out[name] = jnp.asarray(drawn.astype(out[name].dtype))
    for name, factor in factors.items():
        out[name] = (out[name] * factor).astype(out[name].dtype)
    return out
```

```python
from contextlib import ExitStack

import numpy as np
import concourse.bass as bass
from concourse import mybir

F32 = mybir.dt.float32
F16 = mybir.dt.float16
BF16 = mybir.dt.bfloat16
F8 = mybir.dt.float8e4
I32 = mybir.dt.int32
ALU = mybir.AluOpType
ACT = mybir.ActivationFunctionType
AX = mybir.AxisListType
RMAX = bass.bass_isa.ReduceOp.max

P = 128
B, SEQ, H = 4, 512, 512
D = H // 4
KT = H // P
TT = SEQ // P
F0 = 2048
NT0 = F0 // P
F1 = 1376
NT1 = -(-F1 // P)
LASTROWS = F1 - (NT1 - 1) * P
SCALE = float(D) ** -0.5
EPS = 1e-5
BLK = 64
STRIPE = NT1 * P
SBLK = STRIPE // BLK
NSTR = 2 * KT * NT1 * P // STRIPE
PAIR = 2 * F1
PBLK = PAIR // BLK
NATW = 2 * F1 + 32
XS_BITS = 11
XSCALE = 2.0 ** XS_BITS
WBITS = 13
TINY = 2.0 ** -60

NF4 = np.array([-1.0, -0.6961928009986877, -0.5250730514526367, -0.39491748809814453,
                -0.28444138169288635, -0.18477343022823334, -0.09105003625154495, 0.0,
                0.07958029955625534, 0.16093020141124725, 0.24611230194568634,
                0.33791524171829224, 0.44070982933044434, 0.5626170039176941,
                0.7229568362236023, 1.0], np.float32)
BOUNDS = (NF4[:-1] + NF4[1:]) * np.float32(0.5)
STEPS = NF4[1:] - NF4[:-1]
NB = len(BOUNDS)
BIG = 2.0 ** 60

SHARE = [0, 0, 1, 2, 3, 3, 2, 4, 0, 0, 2, 2, 3, 3, 2, 3]


def build(nc, io):
    ctx = ExitStack()
    with ctx:
        def sb(name, shape, dt=F32):
            return ctx.enter_context(nc.sbuf_tensor(name, shape, dt))

        def sem(name):
            return ctx.enter_context(nc.semaphore(name))

        def wait(eng, s, n):
            if not isinstance(n, int) or n > 0:
                eng.wait_ge(s, n)

        x_nat = sb("x_nat", [P, B * TT * H])
        xh = sb("xh", [P, KT, B * SEQ], F16)
        xl = sb("xl", [P, KT, B * SEQ], F16)
        reg_t = sb("reg_t", [P, 12288])
        reg_a = sb("reg_a", [P, 11264])
        reg_n = sb("reg_n", [P, 5632 + 2048])
        sring = sb("sring", [P, 2, SEQ])
        wqkv = sb("wqkv", [P, 1536])
        wo = sb("wo", [P, H])
        bo_bc = sb("bo_bc", [P, H])
        sc_bc = sb("sc_bc", [P, H])
        bv_bc = sb("bv_bc", [P, 2, D])
        idf = sb("idf", [P, P])
        idh = sb("idh", [P, P], F16)
        ones = sb("ones", [P, P])
        bcol = sb("bcol", [P, 2, 3])
        bqs = sb("bqs", [P, 2])
        g_sc = sb("g_sc", [P, NT0])
        u_sc = sb("u_sc", [P, NT0])
        g1_sc = sb("g1_sc", [P, NT1])
        u1_sc = sb("u1_sc", [P, NT1])
        tmp16 = sb("tmp16", [P, 26])
        asum = sb("asum", [P, 12])
        asum3 = sb("asum3", [P, 3])
        thr = sb("thr", [P, 3, 2])
        nmax = sb("nmax", [P, TT])
        rsum = sb("rsum", [P, TT])
        rinv = sb("rinv", [P, TT])
        stats = sb("stats", [P, TT, 6])
        mv = sb("mv", [P, TT, 2])
        nv = sb("nv", [P, 4, TT])
        NAM = 2 * KT * NT1 * 2 + 2 * PBLK
        am = sb("am", [P, NAM])
        rc = sb("rc", [P, NAM])
        rp2 = sb("rp2", [P, 24])
        rinvp2 = sb("rinvp2", [P, 24])
        fac = sb("fac", [P, 12])

        def view(reg, lo, words, dt=F32):
            v = reg[:, lo:lo + words]
            return v if dt == F32 else v.bitcast(dt)

        tg = view(reg_t, 0, 4096, F16).rearrange("p (k f) -> p k f", k=KT)
        tu = view(reg_t, 4096, 4096, F16).rearrange("p (k f) -> p k f", k=KT)
        td = view(reg_t, 8192, 2048, F8).rearrange("p (k f) -> p k f", k=NT0)
        xs = view(reg_t, 10240, 2048)
        tneg = view(reg_t, 10240, 1024, F16)
        w3h = view(reg_t, 0, 2816, F16).rearrange("p (k f) -> p k f", k=NT1)
        w3l = view(reg_t, 2816, 2816, F16).rearrange("p (k f) -> p k f", k=NT1)
        hh1 = view(reg_t, 5632, 2816, F16).rearrange("p (k f) -> p k f", k=NT1)
        hl1 = view(reg_t, 8448, 2816, F16).rearrange("p (k f) -> p k f", k=NT1)
        w12h = view(reg_a, 0, 5632, F16).rearrange("p (s f) -> p s f", f=P)
        w12l = view(reg_a, 5632, 5632, F16).rearrange("p (s f) -> p s f", f=P)
        xT = view(reg_a, 6144, 2048).rearrange("p (k f) -> p k f", k=KT)
        wraw1 = view(reg_a, 8192, 1536)
        raw2 = [view(reg_n, 2048 * i, 2048) for i in range(2)]
        nraw = view(reg_n, 0, STRIPE)
        nacc = view(reg_n, 1408, STRIPE)
        nrel = [view(reg_n, 2816 + 704 * i, 704, BF16) for i in range(2)]
        nhi = view(reg_n, 4224, 704, F16)
        nlo = view(reg_n, 4928, 704, F16)
        n3h = view(reg_n, 4224, NATW // 2, F16)
        n3l = view(reg_n, 4224 + NATW // 2, NATW // 2, F16)
        hring = view(reg_n, 5632, 1024, F16).rearrange("p (s f) -> p s f", s=4)
        lring = view(reg_n, 6656, 1024, F16).rearrange("p (s f) -> p s f", s=4)
        wq_h = view(wqkv, 0, 768, F16)
        wq_l = view(wqkv, 768, 768, F16)

        def attn_bufs(reg, at):
            return dict(qT=view(reg, at, 512), kT=view(reg, at + 512, 512), v=view(reg, at + 1024, 512),
                        oT=view(reg, at + 1536, 512),
                        pr=view(reg, at + 2048, 2048).rearrange("p (t k) -> p t k", t=TT),
                        pT=view(reg, at + 4096, 2048).rearrange("p (t q) -> p t q", t=TT))

        diag3 = view(reg_t, 7680, 2 * P)
        ytmp = view(reg_n, 0, TT * H)
        tq3_groups = [(t, r, s0, ns) for t in range(2) for r in range(2) for s0, ns in ((0, 8), (8, NT1 - 8))]

        bufs = [attn_bufs(reg_a, 0), attn_bufs(reg_t, 5632)]

        bank = [ctx.enter_context(nc.psum_tensor(f"bank{i}", [P, 512], F32)) for i in range(8)]
        bank16 = [t[:, :].bitcast(F16) for t in bank]
        q_ps, k_ps, v_ps, o_ps = bank[0], bank[1], bank[2], bank[3]
        roll = bank[4:8]
        g_ps, u_ps = bank[0:2], bank[2:4]
        y_ps = bank[4:8]
        misc_ps = bank[3]

        s_const = sem("s_const")
        s_w0 = sem("s_w0")
        s_xT = sem("s_xT")
        s_xn = [sem(f"s_xn{i}") for i in range(B)]
        s_raw = [sem("s_raw0"), sem("s_raw1")]
        s_wraw1 = sem("s_wraw1")
        s_w1 = sem("s_w1")
        s_nraw = sem("s_nraw")
        s_out = sem("s_out")
        p_init = sem("p_init")
        p_red = sem("p_red")
        a_sum = sem("a_sum")
        v_raw = sem("v_raw")
        v_init = sem("v_init")
        t_misc = sem("t_misc")
        v_misc = sem("v_misc")

        class AttnSems:

            def __init__(self, tag):
                self.q_mm = sem(tag + "_q_mm")
                self.k_mm = sem(tag + "_k_mm")
                self.v_mm = sem(tag + "_v_mm")
                self.s_mm = sem(tag + "_s_mm")
                self.t_mm = sem(tag + "_t_mm")
                self.o_mm = sem(tag + "_o_mm")
                self.y_mm = sem(tag + "_y_mm")
                self.xt_mm = sem(tag + "_xt_mm")
                self.q_sb = sem(tag + "_q_sb")
                self.k_sb = sem(tag + "_k_sb")
                self.v_sb = sem(tag + "_v_sb")
                self.mx = sem(tag + "_mx")
                self.exp = sem(tag + "_exp")
                self.pt_a = sem(tag + "_pt_a")
                self.pt_d = sem(tag + "_pt_d")
                self.o_sb = sem(tag + "_o_sb")
                self.xb = sem(tag + "_xb")
                self.y_rd = sem(tag + "_y_rd")
                self.ln = sem(tag + "_ln")
                self.xhi = sem(tag + "_xhi")
                self.xlo = sem(tag + "_xlo")

        class FfnSems:

            def __init__(self, tag):
                self.g_mm = sem(tag + "_g_mm")
                self.u_mm = sem(tag + "_u_mm")
                self.d_mm = sem(tag + "_d_mm")
                self.xt_mm = sem(tag + "_xt_mm")
                self.tq_mm = sem(tag + "_tq_mm")
                self.silu = sem(tag + "_silu")
                self.h = sem(tag + "_h")
                self.hi = sem(tag + "_hi")
                self.lo = sem(tag + "_lo")
                self.y_rd = sem(tag + "_y_rd")
                self.ln = sem(tag + "_ln")
                self.xcp = sem(tag + "_xcp")
                self.xhi = sem(tag + "_xhi")
                self.xlo = sem(tag + "_xlo")

        class QuantSems:

            def __init__(self, tag):
                self.xn = sem(tag + "_xn")
                self.rel = sem(tag + "_rel")
                self.stt = sem(tag + "_stt")
                self.dq = sem(tag + "_dq")
                self.hi = sem(tag + "_hi")
                self.lo = sem(tag + "_lo")
                self.tq_mm = sem(tag + "_tq_mm")
                self.tq_a = sem(tag + "_tq_a")
                self.tq_d = sem(tag + "_tq_d")

        at = [AttnSems(f"a{l}") for l in range(2)]
        ff = [FfnSems(f"f{l}") for l in range(2)]
        nf = QuantSems("nf")
        n3 = QuantSems("n3")

        stream = ([("sum", m, c) for m in (0, 1) for c in range(4)]
                  + [("tern", 0, c) for c in range(4)] + [("sum", 2, c) for c in range(4)]
                  + [("tern", 1, c) for c in range(4)] + [("tern", 2, c) for c in range(4)]
                  + [("amax", m, c) for m in range(3) for c in range(4)])
        n_act = {n: i for i, n in enumerate([n for n, s in enumerate(stream) if s[0] == "sum"])}
        n_dve = {n: i for i, n in enumerate([n for n, s in enumerate(stream) if s[0] != "sum"])}
        w3_part = [(t, half, half * SBLK, SBLK if half == 0 else PBLK - SBLK) for t in range(2) for half in range(2)]

        def chunk_src(kind, m, c):
            if kind == "amax":
                if m < 2:
                    return io["w12n"][4 * m + c], STRIPE
                t, _, b0, nb = w3_part[c]
                return io["w3n"][t][:, b0 * BLK:(b0 + nb) * BLK], nb * BLK
            return io["tern"][m][c], 2048

        def am_cols(m, c):
            if m < 2:
                return (4 * m + c) * SBLK, SBLK
            t, _, b0, nb = w3_part[c]
            return 8 * SBLK + t * PBLK + b0, nb

        def chunk_wait(eng, n):
            eng.wait_ge(s_raw[n % 2], 16 * (n // 2 + 1))

        block = ctx.enter_context(nc.Block())

        @block.sync
        def _(sp):
            sp.dma_start(wqkv[:, :].rearrange("p (k f) -> p k f", k=KT), io["wqkv"][0]).then_inc(s_w0, 16)
            sp.dma_start(bcol[:, :, :], io["bcol"]).then_inc(s_const, 16)
            sp.dma_start(bv_bc[:, 0, :], io["bv"][0]).then_inc(s_const, 16)
            sp.dma_start(bv_bc[:, 1, :], io["bv"][1]).then_inc(s_const, 16)
            sp.dma_start(bo_bc[:, :], io["bo"][0]).then_inc(s_const, 16)
            sp.dma_start(wo[:, :], io["wo"][0]).then_inc(s_w0, 16)
            sp.dma_start(g_sc[:, :], io["gsc"]).then_inc(s_const, 16)
            sp.dma_start(u_sc[:, :], io["usc"]).then_inc(s_const, 16)
            sp.dma_start(sc_bc[:, :], io["dsc"]).then_inc(s_const, 16)
            sp.dma_start(wraw1, io["wqkv1"]).then_inc(s_wraw1, 16)
            for b in range(B):
                sp.dma_start(x_nat[:, b * TT * H:(b + 1) * TT * H].rearrange("p (t f) -> p t f", t=TT),
                             io["xn"][b]).then_inc(s_xn[b], 16)
            for n, (kind, m, c) in enumerate(stream):
                if n >= 2:
                    if n - 2 in n_act:
                        sp.wait_ge(a_sum, n_act[n - 2] + 1)
                    else:
                        sp.wait_ge(v_raw, n_dve[n - 2] + 1)
                src, w = chunk_src(kind, m, c)
                dst = raw2[n % 2][:, 0:w]
                if len(src.shape) == 3:
                    dst = dst.rearrange("p (k f) -> p k f", k=src.shape[1])
                sp.dma_start(dst, src).then_inc(s_raw[n % 2], 16)
            sp.wait_ge(at[0].y_mm, B * TT)
            sp.dma_start(wo[:, :], io["wo"][1]).then_inc(s_w1, 16)
            sp.wait_ge(at[0].xb, B * TT)
            sp.dma_start(bo_bc[:, :], io["bo"][1]).then_inc(s_w1, 16)
            sp.wait_ge(v_raw, len(n_dve))
            sp.dma_start(nraw, io["w12n"][0]).then_inc(s_nraw, 16)
            with sp.Fori(1, NSTR) as s:
                sp.wait_ge(nf.rel, s * NB)
                sp.dma_start(nraw, io["w12n"][bass.ds(s, 1), :, :].rearrange("a p f -> p (a f)")).then_inc(s_nraw, 16)
            for c, (t, half, b0, nb) in enumerate(w3_part):
                if c == 0:
                    sp.wait_ge(nf.rel, NSTR * NB)
                else:
                    sp.wait_ge(n3.rel, c * NB)
                sp.dma_start(nraw[:, 0:nb * BLK], io["w3n"][t][:, b0 * BLK:(b0 + nb) * BLK]).then_inc(s_nraw, 16)
            with sp.Fori(0, B) as b:
                sp.wait_ge(ff[1].ln, b + 1)
                sp.dma_start(io["out"][bass.ds(b, 1), :, :, :].rearrange("a p t f -> p (a t) f"),
                             x_nat[:, bass.ds(b * (TT * H), TT * H)].rearrange("p (t f) -> p t f", t=TT)
                             ).then_inc(s_out, 16)
            sp.wait_ge(s_out, 16 * B)

        @block.gpsimd
        def _(pool):
            pool.memset(idf[:, :], 0.0).then_inc(p_init, 1)
            pool.memset(ones[:, :], 1.0).then_inc(p_init, 1)
            pool.wait_ge(p_init, 2)
            pool.affine_select(out=idf[:, :], in_=idf[:, :], compare_op=ALU.not_equal, fill=1.0, base=0,
                               pattern=[[-1, P]], channel_multiplier=1).then_inc(p_init, 1)
            pool.wait_ge(p_init, 3)
            pool.tensor_copy(idh[:, :], idf[:, :]).then_inc(p_init, 1)
            pool.wait_ge(v_init, 1)
            pool.partition_all_reduce(fac[:, 1:2], fac[:, 0:1], P, RMAX).then_inc(p_red, 1)
            pool.wait_ge(v_init, 3)
            pool.partition_all_reduce(fac[:, 5:6], fac[:, 4:5], P, RMAX).then_inc(p_red, 1)

            def add_bo(l, b):
                a = at[l]
                for t in range(TT):
                    v = x_nat[:, (b * TT + t) * H:(b * TT + t + 1) * H]
                    pool.tensor_tensor(v, v, bo_bc[:, :], ALU.add).then_inc(a.xb, 1)

            pool.wait_ge(s_const, 16 * 7)
            for b in range(B):
                pool.wait_ge(s_xn[b], 16)
                add_bo(0, b)
            pool.wait_ge(v_init, 5)
            pool.partition_all_reduce(fac[:, 9:10], fac[:, 8:9], P, RMAX).then_inc(p_red, 1)

            def lo0(n, j):
                f = ff[0]
                pool.wait_ge(f.hi, n + 1)
                pool.tensor_tensor(lring[:, j % 4, :], sring[:, j % 2, :], hring[:, j % 4, :],
                                   ALU.subtract).then_inc(f.lo, 1)

            def norm_stripe(s):
                pool.wait_ge(s_nraw, 16 * (s + 1))
                v = nraw.rearrange("p (b c) -> p b c", c=BLK)
                r = rc[:, bass.ds(s * SBLK, SBLK)].unsqueeze(2).to_broadcast([P, SBLK, BLK])
                pool.tensor_tensor(v, v, r, ALU.mult).then_inc(nf.xn, 1)

            def copy_x(b):
                pool.wait_ge(ff[0].ln, b + 1)
                pool.tensor_copy(x_nat[:, bass.ds(b * (TT * H), TT * H)], xs).then_inc(ff[0].xcp, 1)

            pool.wait_ge(v_init, 5)

            def body(b, first):
                for j in range(NT0):
                    if j == 4 and not first:
                        copy_x(b - 1)
                    lo0(b * NT0 + j, j)
                    if j == 0:
                        norm_stripe(2 * b)
                    if j == 8:
                        norm_stripe(2 * b + 1)
            body(0, True)
            with pool.Fori(1, B) as b:
                body(b, False)
            copy_x(B - 1)

            a = at[1]
            pool.wait_ge(s_w1, 32)
            pool.wait_ge(ff[0].xcp, B)
            for b in range(B):
                pool.wait_ge(ff[0].xlo, 4 * (b + 1))
                add_bo(1, b)
            def norm_w3():
                for c, (t, half, b0, nb) in enumerate(w3_part):
                    pool.wait_ge(s_nraw, 16 * (NSTR + c + 1))
                    v = nraw[:, 0:nb * BLK].rearrange("p (b c) -> p b c", c=BLK)
                    k0 = 8 * SBLK + t * PBLK + b0
                    r = rc[:, k0:k0 + nb].unsqueeze(2).to_broadcast([P, nb, BLK])
                    pool.tensor_tensor(v, v, r, ALU.mult).then_inc(n3.xn, 1)

            def body1(b):
                f = ff[1]
                for j in range(NT1):
                    n = b * NT1 + j
                    pool.wait_ge(f.hi, n + 1)
                    pool.tensor_tensor(hl1[:, j, :], sring[:, j % 2, :],
                                       hh1[:, j, :], ALU.subtract).then_inc(f.lo, 1)
            body1(0)
            norm_w3()
            with pool.Fori(1, B) as b:
                body1(b)

        @block.scalar
        def _(act):
            def load_xT(b):
                act.dma_start(xT, io["xT"][b]).then_inc(s_xT, 16)

            load_xT(0)
            act.wait_ge(v_init, 2)

            def sum_abs(m):
                for c in range(4):
                    n = stream.index(("sum", m, c))
                    chunk_wait(act, n)
                    act.activation(raw2[n % 2], raw2[n % 2], ACT.Abs,
                                   accum_out=asum[:, 4 * m + c:4 * m + c + 1]).then_inc(a_sum, 1)

            def q_evac(l, b):
                a, u = at[l], bufs[l]
                act.wait_ge(a.q_mm, b + 1)
                sc = SCALE if l == 0 else fac[:, 7:8]
                act.activation(u["qT"], q_ps[:, :], ACT.Identity, bias=bqs[:, l:l + 1], scale=sc).then_inc(a.q_sb, 1)

            def x_hi(a, kt, src, b):
                act.activation(xh[:, kt, bass.ds(b * SEQ, SEQ)] if not isinstance(b, int) else
                               xh[:, kt, b * SEQ:(b + 1) * SEQ], src[:, :], ACT.Copy, scale=XSCALE).then_inc(a.xhi, 1)

            def attention(l):
                a, u = at[l], bufs[l]
                q_evac(l, 0)
                if l == 0:
                    act.wait_ge(a.v_mm, 1)
                    load_xT(1)
                for b in range(B):
                    for t in range(TT):
                        act.wait_ge(a.mx, 4 * b + t + 1)
                        wait(act, a.t_mm, 4 * b)
                        act.activation(u["pr"][:, t, :], roll[t][:, :], ACT.Exp, bias=nmax[:, t:t + 1],
                                       accum_out=rsum[:, t:t + 1]).then_inc(a.exp, 1)
                    if b + 1 < B:
                        q_evac(l, b + 1)
                        if l == 0 and b + 2 < B:
                            act.wait_ge(a.v_mm, b + 2)
                            load_xT(b + 2)
                    if b >= 1:
                        for kt in range(KT):
                            act.wait_ge(a.xt_mm, 4 * (b - 1) + kt + 1)
                            x_hi(a, kt, roll[kt], b - 1)
                    if l == 1 and b == 0:
                        act.wait_ge(ff[0].xcp, B)
                    for kt in (0, 2):
                        act.wait_ge(a.t_mm, 4 * b + kt + 1)
                        act.activation(u["pT"][:, kt, :], roll[kt][:, :], ACT.Copy).then_inc(a.pt_a, 1)
                    act.wait_ge(a.o_mm, b + 1)
                    act.activation(u["oT"], o_ps[:, :], ACT.Copy).then_inc(a.o_sb, 1)
                    if l == 0 and b == 0:
                        sum_abs(0)
                        sum_abs(1)
                    if l == 0 and b == 1:
                        sum_abs(2)
                for kt in range(KT):
                    act.wait_ge(a.xt_mm, 4 * (B - 1) + kt + 1)
                    x_hi(a, kt, roll[kt], B - 1)

            def ffn0():
                f = ff[0]

                def tq_hi(s, j):
                    e = (j + 1) % 2
                    for i, (pb, s0, ns) in enumerate(((g_ps[e], 0, 8), (g_ps[1 - e], 8, 3))):
                        act.wait_ge(f.tq_mm, 4 * s + (1, 3)[i])
                        act.activation(w12h[:, bass.ds(s * NT1 + s0, ns), :],
                                       pb[:, :].bitcast(F16)[:, 0:ns * P].rearrange("p (s f) -> p s f", f=P),
                                       ACT.Copy).then_inc(nf.tq_a, 1)

                def body(b, first):
                    for j in range(NT0):
                        n = b * NT0 + j
                        half = j // 8
                        s = 2 * b + half
                        act.wait_ge(f.g_mm, n + 1)
                        wait(act, f.lo, n - 1 if not first or j >= 2 else 0)
                        act.activation(sring[:, j % 2, :], g_ps[j % 2][:, :], ACT.Silu,
                                       scale=g_sc[:, j:j + 1]).then_inc(f.silu, 1)
                        k0 = sum(SHARE[8 * half:j])
                        for k in range(k0, k0 + SHARE[j]):
                            if k == 0:
                                act.wait_ge(nf.xn, s + 1)
                            m = s * NB + k
                            if not (first and half == 0 and k < 2):
                                act.wait_ge(nf.stt, m - 1)
                            act.activation(nrel[(k + half) % 2], nraw, ACT.Relu, scale=BIG,
                                           bias=-BIG * float(BOUNDS[k])).then_inc(nf.rel, 1)
                        act.wait_ge(f.h, n + 1)
                        wait(act, f.d_mm, n - 3 if not first or j >= 4 else 0)
                        act.activation(hring[:, j % 4, :], sring[:, j % 2, :], ACT.Copy).then_inc(f.hi, 1)
                        if j == 8 or (j == 0 and not first):
                            sd = s - 1
                            act.wait_ge(nf.dq, sd + 1)
                            wait(act, f.tq_mm, 4 * sd if not (first and j == 8) else 0)
                            act.activation(nhi, nacc, ACT.Copy).then_inc(nf.hi, 1)
                        if j == 2 and not first:
                            tq_hi(2 * b - 1, j)
                        if j == 10:
                            tq_hi(2 * b, j)
                        if j == 6 and not first:
                            for kt, pb in enumerate((g_ps[1], u_ps[1], g_ps[0], u_ps[0])):
                                act.wait_ge(f.xt_mm, 4 * (b - 1) + kt + 1)
                                x_hi(f, kt, pb, b - 1)
                body(0, True)
                with act.Fori(1, B) as b:
                    body(b, False)
                act.wait_ge(nf.dq, NSTR)
                act.wait_ge(f.tq_mm, 4 * (NSTR - 1))
                act.activation(nhi, nacc, ACT.Copy).then_inc(nf.hi, 1)
                tq_hi(NSTR - 1, NT0 - 1)
                for kt in range(KT):
                    act.wait_ge(f.xt_mm, 4 * (B - 1) + kt + 1)
                    x_hi(f, kt, y_ps[kt], B - 1)

            def relu3(c, k, w):
                if k == 0:
                    act.wait_ge(n3.xn, c + 1)
                m = c * NB + k
                wait(act, n3.stt, m - 1)
                act.activation(nrel[m % 2][:, 0:w], nraw[:, 0:w], ACT.Relu, scale=BIG,
                               bias=-BIG * float(BOUNDS[k])).then_inc(n3.rel, 1)

            def w3_quant():
                for c, (t, half, b0, nb) in enumerate(w3_part):
                    w = nb * BLK
                    for k in range(NB):
                        relu3(c, k, w)
                    act.wait_ge(n3.dq, c + 1)
                    if half == 0:
                        wait(act, n3.tq_mm, 8 * t)
                    act.activation(n3h[:, half * STRIPE:half * STRIPE + w], nacc[:, 0:w], ACT.Copy).then_inc(n3.hi, 1)
                    if half:
                        for i in range(4 * t, 4 * t + 4):
                            _, r, s0, ns = tq3_groups[i]
                            act.wait_ge(n3.tq_mm, 2 * i + 1)
                            act.activation(w3h[:, s0:s0 + ns, (2 * t + r) * P:(2 * t + r + 1) * P],
                                           y_ps[(2 * i) % 4][:, :].bitcast(F16)[:, 0:ns * P].rearrange(
                                               "p (s f) -> p s f", f=P), ACT.Copy).then_inc(n3.tq_a, 1)

            def ffn1():
                f = ff[1]

                def body(b, first):
                    for j in range(NT1):
                        n = b * NT1 + j
                        act.wait_ge(f.g_mm, n + 1)
                        if not first or j >= 2:
                            act.wait_ge(f.lo, n - 1 if j else n)
                        act.activation(sring[:, j % 2, :], g_ps[j % 2][:, :], ACT.Silu,
                                       scale=g1_sc[:, j:j + 1]).then_inc(f.silu, 1)
                        act.wait_ge(f.h, n + 1)
                        act.activation(hh1[:, j, :], sring[:, j % 2, :], ACT.Copy).then_inc(f.hi, 1)
                        if first and j == NT1 - 1:
                            w3_quant()
                body(0, True)
                with act.Fori(1, B) as b:
                    body(b, False)

            attention(0)
            ffn0()
            attention(1)
            ffn1()

        @block.tensor
        def _(pe):
            def project(l, b):
                a = at[l]
                if l == 0:
                    pe.wait_ge(s_xT, 16 * (b + 1))
                    w = wqkv[:, :].rearrange("p (k f) -> p k f", k=KT)
                    passes = [(w, xT, 0)]
                else:
                    wh = wq_h.rearrange("p (k f) -> p k f", k=KT)
                    wl = wq_l.rearrange("p (k f) -> p k f", k=KT)
                    c0 = b * SEQ
                    pe.wait_ge(ff[0].xlo, 4 * (b + 1))
                    passes = [(wh, xh, c0), (wh, xl, c0), (wl, xh, c0)]
                np_ = KT * len(passes)
                for part, (ps, mm, used) in enumerate(((q_ps, a.q_mm, a.q_sb), (k_ps, a.k_mm, a.k_sb))):
                    wait(pe, used, b)
                    i = 0
                    for kt in range(KT):
                        for w, x, c0 in passes:
                            m = pe.matmul(ps[:, :], w[:, kt, part * D:(part + 1) * D], x[:, kt, c0:c0 + SEQ],
                                          start=(i == 0), stop=(i == np_ - 1))
                            i += 1
                    m.then_inc(mm, 1)
                wait(pe, a.v_sb, b)
                for t in range(TT):
                    i = 0
                    for kt in range(KT):
                        for w, x, c0 in passes:
                            m = pe.matmul(v_ps[:, t * D:(t + 1) * D], x[:, kt, c0 + t * P:c0 + (t + 1) * P],
                                          w[:, kt, 2 * D:3 * D], start=(i == 0), stop=(i == np_ - 1))
                            i += 1
                m.then_inc(a.v_mm, 1)

            def transpose_x(src, done, banks, kts):
                for kt in kts:
                    for t in range(TT):
                        m = pe.transpose(banks[kt][:, t * P:(t + 1) * P], src[:, t * H + kt * P:t * H + (kt + 1) * P],
                                         idf[:, :])
                    m.then_inc(done, 1)

            def attention(l):
                a, u = at[l], bufs[l]
                project(l, 0)
                for b in range(B):
                    pe.wait_ge(a.q_sb, b + 1)
                    pe.wait_ge(a.k_sb, b + 1)
                    if l == 1 and b == 0:
                        pe.wait_ge(ff[0].xlo, 4 * B)
                    for t in range(TT):
                        wait(pe, a.y_rd, 4 * (b - 1) + t + 1)
                        pe.matmul(roll[t][:, :], u["qT"][:, t * P:(t + 1) * P], u["kT"], start=True,
                                  stop=True).then_inc(a.s_mm, 1)
                    if b + 1 < B:
                        project(l, b + 1)
                    if l == 0 and b in (1, 3):
                        pe.wait_ge(v_misc, b)
                        pe.wait_ge(a.o_sb, b)
                        pe.matmul(misc_ps[:, 0:3], ones[:, :], asum3[:, :], start=True, stop=True).then_inc(t_misc, 1)
                    if b >= 1:
                        pe.wait_ge(a.ln, b)
                        for kt in range(KT):
                            pe.wait_ge(a.exp, 4 * b + kt + 1)
                            transpose_x(x_nat[:, (b - 1) * TT * H:b * TT * H], a.xt_mm, roll, [kt])
                    pe.wait_ge(a.exp, 4 * b + 4)
                    for kt in range(KT):
                        wait(pe, a.xlo, 4 * (b - 1) + kt + 1)
                        for t in range(TT):
                            m = pe.transpose(roll[kt][:, t * P:(t + 1) * P], u["pr"][:, t, kt * P:(kt + 1) * P],
                                             idf[:, :])
                        m.then_inc(a.t_mm, 1)
                    pe.wait_ge(a.v_sb, b + 1)
                    wait(pe, a.o_sb, b)
                    if l == 0 and b in (1, 3):
                        pe.wait_ge(v_misc, b + 1)
                    for kt in range(KT):
                        pe.wait_ge((a.pt_a, a.pt_d)[kt % 2], 2 * b + kt // 2 + 1)
                        m = pe.matmul(o_ps[:, :], u["v"][:, kt * D:(kt + 1) * D], u["pT"][:, kt, :],
                                      start=(kt == 0), stop=(kt == KT - 1))
                    m.then_inc(a.o_mm, 1)
                    pe.wait_ge(a.o_sb, b + 1)
                    for t in range(TT):
                        pe.matmul(roll[t][:, :], u["oT"][:, t * P:(t + 1) * P], wo[:, :], start=True,
                                  stop=True).then_inc(a.y_mm, 1)
                pe.wait_ge(a.ln, B)
                for kt in range(KT):
                    transpose_x(x_nat[:, (B - 1) * TT * H:B * TT * H], a.xt_mm, roll, [kt])

            def ffn0():
                f = ff[0]

                def down(n, j):
                    pe.wait_ge(f.lo, n + 1)
                    pe.ldweights(hring[:, j % 4, 0:P], tile_position=(0, 0))
                    pe.wait_ge(v_raw, 12)
                    for part, ring in enumerate((hring, lring)):
                        for t in range(TT):
                            m = pe.matmul(y_ps[t][:, :], ring[:, j % 4, t * P:(t + 1) * P], td[:, j, :],
                                          start=(j == 0 and part == 0), stop=(j == NT0 - 1 and part == 1))
                    m.then_inc(f.d_mm, 1)

                def tq(s, j, n, full):
                    e = (j + 1) % 2
                    pe.wait_ge(nf.lo, s + 1)
                    for i, (pb, src, s0, ns, used, d) in enumerate(
                            ((g_ps[e], nhi, 0, 8, f.silu, 0), (u_ps[e], nlo, 0, 8, f.h, 0),
                             (g_ps[1 - e], nhi, 8, 3, f.silu, 1), (u_ps[1 - e], nlo, 8, 3, f.h, 1))):
                        pe.wait_ge(used, n + d)
                        for k in range(ns):
                            m = pe.transpose(pb[:, :].bitcast(F16)[:, k * P:(k + 1) * P],
                                             src[:, (s0 + k) * P:(s0 + k + 1) * P], idh[:, :])
                        m.then_inc(f.tq_mm, 1)

                def body(b, first):
                    c0 = b * SEQ
                    for j in range(NT0):
                        n = b * NT0 + j
                        if j == 0:
                            pe.wait_ge(at[0].xlo, 4 * (b + 1))
                            pe.wait_ge(v_raw, 8)
                        for ps, w, mm, used, tqs, k in ((g_ps[j % 2], tg, f.g_mm, f.silu, nf.tq_a, 0),
                                                        (u_ps[j % 2], tu, f.u_mm, f.h, nf.tq_d, 1)):
                            if not first or j >= 2:
                                pe.wait_ge(used, n - 1)
                            if j in (11, 12):
                                pe.wait_ge(tqs, 2 * (2 * b) + j - 10)
                            if j in (3, 4) and not first:
                                pe.wait_ge(tqs, 2 * (2 * b - 1) + j - 2)
                            if j in (7, 8) and not first:
                                pe.wait_ge(f.xlo, 4 * (b - 1) + 2 * (j - 7) + k + 1)
                            i = 0
                            for kt in range(KT):
                                for x in (xh, xl):
                                    xv = x[:, kt, bass.ds(c0, SEQ)] if not first else x[:, kt, 0:SEQ]
                                    m = pe.matmul(ps[:, :], w[:, kt, j * P:(j + 1) * P], xv,
                                                  start=(i == 0), stop=(i == 2 * KT - 1))
                                    i += 1
                            m.then_inc(mm, 1)
                        if j >= 2 or not first:
                            if j == 2:
                                if first:
                                    pe.wait_ge(at[0].xlo, 4 * B)
                                else:
                                    pe.wait_ge(f.y_rd, 4 * b)
                            down(n - 2, (j - 2) % NT0)
                        if j == 2 and not first:
                            tq(2 * b - 1, j, n, True)
                        if j == 10:
                            tq(2 * b, j, n, True)
                        if j == 6 and not first:
                            pe.wait_ge(f.ln, b)
                            for kt, (pb, used, d) in enumerate(((g_ps[1], f.silu, 0), (u_ps[1], f.h, 0),
                                                                (g_ps[0], f.silu, 1), (u_ps[0], f.h, 1))):
                                pe.wait_ge(used, n + d)
                                transpose_x(xs, f.xt_mm, {kt: pb}, [kt])
                body(0, True)
                with pe.Fori(1, B) as b:
                    body(b, False)
                for j in (NT0 - 2, NT0 - 1):
                    down((B - 1) * NT0 + j, j)
                tq(NSTR - 1, NT0 - 1, B * NT0 - 1, True)
                pe.wait_ge(f.ln, B)
                transpose_x(xs, f.xt_mm, y_ps, range(KT))

            def ffn1():
                f = ff[1]

                def body(b, first):
                    c0 = b * SEQ
                    for j in range(NT1):
                        n = b * NT1 + j
                        if j == 0:
                            pe.wait_ge(at[1].xlo, 4 * (b + 1))
                        for ps, s0, mm, used in ((g_ps[j % 2], 0, f.g_mm, f.silu),
                                                 (u_ps[j % 2], KT * NT1, f.u_mm, f.h)):
                            if not first or j >= 2:
                                pe.wait_ge(used, n - 1 if j else n)
                            i = 0
                            for kt in range(KT):
                                for w, x in ((w12h, xh), (w12h, xl), (w12l, xh)):
                                    xv = x[:, kt, bass.ds(c0, SEQ)] if not first else x[:, kt, 0:SEQ]
                                    m = pe.matmul(ps[:, :], w[:, s0 + KT * j + kt, :], xv,
                                                  start=(i == 0), stop=(i == 3 * KT - 1))
                                    i += 1
                            m.then_inc(mm, 1)
                    if first:
                        pe.wait_ge(at[1].xlo, 4 * B)
                        transpose_w3()
                    else:
                        pe.wait_ge(f.y_rd, 4 * b)
                    for j in range(NT1):
                        n = b * NT1 + j
                        rows = P if j < NT1 - 1 else LASTROWS
                        pe.wait_ge(f.lo, n + 1)
                        for part, (hp, wp) in enumerate(((hh1, w3h), (hh1, w3l), (hl1, w3h))):
                            for t in range(TT):
                                m = pe.matmul(y_ps[t][:, :], hp[0:rows, j, t * P:(t + 1) * P], wp[0:rows, j, :],
                                              start=(j == 0 and part == 0), stop=(j == NT1 - 1 and part == 2))
                        m.then_inc(f.d_mm, 1)

                def transpose_w3():
                    for i, (t, r, s0, ns) in enumerate(tq3_groups):
                        if i % 4 == 0:
                            pe.wait_ge(n3.lo, 2 * (i // 4) + 2)
                        for part, (src, used) in enumerate(((n3h, n3.tq_a), (n3l, n3.tq_d))):
                            wait(pe, used, i - 1)
                            for k in range(ns):
                                c = r * F1 + (s0 + k) * P
                                m = pe.transpose(y_ps[(2 * i + part) % 4][:, :].bitcast(F16)[:, k * P:(k + 1) * P],
                                                 src[:, c:c + P], idh[:, :])
                            m.then_inc(n3.tq_mm, 1)
                    for used in (n3.tq_a, n3.tq_d):
                        pe.wait_ge(used, len(tq3_groups))

                body(0, True)
                with pe.Fori(1, B) as b:
                    body(b, False)

            pe.wait_ge(p_init, 4)
            pe.wait_ge(s_w0, 32)
            attention(0)
            ffn0()
            pe.wait_ge(nf.tq_a, 2 * NSTR)
            pe.wait_ge(nf.tq_d, 2 * NSTR)
            pe.wait_ge(v_init, 6)
            for t in range(2):
                m = pe.matmul(misc_ps[:, t * P:(t + 1) * P], ones[:, :], diag3[:, t * P:(t + 1) * P],
                              start=True, stop=True)
            m.then_inc(t_misc, 1)
            pe.wait_ge(v_init, 7)
            pe.wait_ge(s_w1, 32)
            attention(1)
            ffn1()

        @block.vector
        def _(dve):
            TS, TTo, STT = dve.tensor_scalar, dve.tensor_tensor, dve.scalar_tensor_tensor

            def pow2_of(out, src):
                TS(out, src, TINY, None, ALU.max)
                dve.drain()
                o = out.bitcast(I32)
                TS(o, o, 0x7F800000, None, ALU.bitwise_and)
                dve.drain()

            def inverse_pow2(out, p2, bits):
                m = TS(out.bitcast(I32), p2.bitcast(I32), -1.0, float((254 + bits) << 23), ALU.mult, ALU.add)
                dve.drain()
                return m

            def tern(m, c):
                n = stream.index(("tern", m, c))
                chunk_wait(dve, n)
                raw = raw2[n % 2]
                dst = ((tg, tu)[m][:, c, :] if m < 2 else
                       td[:, 4 * c:4 * c + 4, :].rearrange("p k f -> p (k f)"))
                neg = tneg
                TS(neg, raw, thr[:, m, 1:2], None, ALU.is_lt)
                dve.drain()
                STT(out=dst, in0=raw, scalar=thr[:, m, 0:1], in1=neg, op0=ALU.is_gt,
                    op1=ALU.subtract, **({"saturate": False} if m == 2 else {})).then_inc(v_raw, 1)
                dve.drain()

            def absmax(m, c):
                n = stream.index(("amax", m, c))
                chunk_wait(dve, n)
                k0, nb = am_cols(m, c)
                dve.tensor_reduce(am[:, k0:k0 + nb], raw2[n % 2][:, 0:nb * BLK].rearrange("p (b c) -> p b c", c=BLK),
                                  AX.X, ALU.max, apply_absolute_value=True).then_inc(v_raw, 1)

            def thresholds(ms, count, done):
                dve.wait_ge(a_sum, 4 * count)
                dve.tensor_reduce(asum3[:, ms[0]:ms[-1] + 1], asum[:, 4 * ms[0]:4 * ms[-1] + 4].rearrange(
                    "p (m c) -> p m c", c=4), AX.X, ALU.add).then_inc(v_misc, 1)
                dve.wait_ge(t_misc, done)
                for m in ms:
                    TS(thr[:, m, 0:1], misc_ps[:, m:m + 1], 1.0 / (F0 * H), float(np.float32(0.7)), ALU.mult, ALU.mult)
                dve.drain()
                for m in ms:
                    last = TS(thr[:, m, 1:2], thr[:, m, 0:1], -1.0, None, ALU.mult)
                last.then_inc(v_misc, 1)
                dve.drain()

            def layernorm(src, dst, done):
                for t in range(TT):
                    dve.bn_stats(stats[:, t, :], src(t))
                dve.drain()
                for t in range(TT):
                    dve.bn_aggr(mv[:, t, :], stats[:, t, :])
                dve.drain()
                var, y, z = nv[:, 0, :], nv[:, 1, :], nv[:, 2, :]
                TS(var, mv[:, :, 1], EPS, None, ALU.add)
                dve.drain()
                TS(y.bitcast(I32), var.bitcast(I32), 1, None, ALU.logical_shift_right)
                dve.drain()
                TS(y.bitcast(I32), y.bitcast(I32), -1.0, float(0x5F3759DF), ALU.mult, ALU.add)
                dve.drain()
                for _ in range(3):
                    STT(out=z, in0=y, scalar=-0.5, in1=y, op0=ALU.mult, op1=ALU.mult)
                    dve.drain()
                    TTo(z, z, var, ALU.mult)
                    dve.drain()
                    STT(out=y, in0=z, scalar=1.5, in1=y, op0=ALU.add, op1=ALU.mult)
                    dve.drain()
                for t in range(TT):
                    m = TS(dst(t), src(t), mv[:, t, 0:1], y[:, t:t + 1], ALU.subtract, ALU.mult)
                m.then_inc(done, 1)

            def x_lo(a, kt, src, b):
                c = slice(b * SEQ, (b + 1) * SEQ) if isinstance(b, int) else bass.ds(b * SEQ, SEQ)
                STT(out=xl[:, kt, c], in0=src[:, :], scalar=XSCALE, in1=xh[:, kt, c], op0=ALU.mult,
                    op1=ALU.subtract).then_inc(a.xlo, 1)

            def attention(l):
                a, u = at[l], bufs[l]

                def k_evac(b):
                    dve.wait_ge(a.k_mm, b + 1)
                    if l == 0:
                        TS(u["kT"], k_ps[:, :], bcol[:, 0, 1:2], None, ALU.add).then_inc(a.k_sb, 1)
                    else:
                        TS(u["kT"], k_ps[:, :], fac[:, 6:7], bcol[:, 1, 1:2], ALU.mult, ALU.add).then_inc(a.k_sb, 1)

                def v_evac(b):
                    dve.wait_ge(a.v_mm, b + 1)
                    wait(dve, a.o_mm, b)
                    out = u["v"].rearrange("p (t f) -> p t f", t=TT)
                    src = v_ps[:, :].rearrange("p (t f) -> p t f", t=TT)
                    bias = bv_bc[:, l, :].unsqueeze(1).to_broadcast([P, TT, D])
                    if l == 0:
                        TTo(out, src, bias, ALU.add).then_inc(a.v_sb, 1)
                    else:
                        STT(out=out, in0=src, scalar=fac[:, 6:7], in1=bias, op0=ALU.mult,
                            op1=ALU.add).then_inc(a.v_sb, 1)

                k_evac(0)
                v_evac(0)
                for b in range(B):
                    for t in range(TT):
                        dve.wait_ge(a.s_mm, 4 * b + t + 1)
                        dve.tensor_reduce(nmax[:, t:t + 1], roll[t][:, :], AX.X, ALU.max, negate=True).then_inc(a.mx, 1)
                    if b + 1 < B:
                        k_evac(b + 1)
                    if l == 0 and b == 1:
                        thresholds((0, 1), 2, 1)
                    if l == 0 and b == 3:
                        thresholds((2,), 3, 2)
                    if l == 0 and b >= 1:
                        for c in range(3):
                            tern(b - 1, c)
                    if b >= 1:
                        for kt in range(KT):
                            dve.wait_ge(a.xhi, 4 * (b - 1) + kt + 1)
                            x_lo(a, kt, roll[kt], b - 1)
                    if l == 1 and b == 0:
                        dve.wait_ge(ff[0].xcp, B)
                    for kt in (1, 3):
                        dve.wait_ge(a.t_mm, 4 * b + kt + 1)
                        dve.tensor_copy(u["pT"][:, kt, :], roll[kt][:, :]).then_inc(a.pt_d, 1)
                    if b + 1 < B:
                        v_evac(b + 1)
                    dve.wait_ge(a.exp, 4 * b + 4)
                    dve.reciprocal(rinv[:, :], rsum[:, :])
                    dve.drain()

                    def tile(t):
                        return x_nat[:, (b * TT + t) * H:(b * TT + t + 1) * H]
                    for t in range(TT):
                        dve.wait_ge(a.y_mm, 4 * b + t + 1)
                        dve.wait_ge(a.xb, 4 * b + t + 1)
                        STT(out=tile(t), in0=roll[t][:, :], scalar=rinv[:, t:t + 1], in1=tile(t), op0=ALU.mult,
                            op1=ALU.add).then_inc(a.y_rd, 1)
                    dve.drain()
                    layernorm(tile, tile, a.ln)
                    if l == 0 and b >= 1:
                        tern(b - 1, 3)
                for kt in range(KT):
                    dve.wait_ge(a.xhi, 4 * (B - 1) + kt + 1)
                    x_lo(a, kt, roll[kt], B - 1)

            def stt(ph, k, w, slot, m):
                dve.wait_ge(ph.rel, m + 1)
                if k == 0:
                    TS(nacc[:, 0:w], nrel[slot][:, 0:w], float(STEPS[0]), float(NF4[0]), ALU.min,
                       ALU.add).then_inc(ph.stt, 1)
                else:
                    STT(out=nacc[:, 0:w], in0=nrel[slot][:, 0:w], scalar=float(STEPS[k]), in1=nacc[:, 0:w],
                        op0=ALU.min, op1=ALU.add).then_inc(ph.stt, 1)
                dve.drain()

            def dequant(ph, scales, nb):
                v = nacc[:, 0:nb * BLK].rearrange("p (b c) -> p b c", c=BLK)
                TTo(v, v, scales.unsqueeze(2).to_broadcast([P, nb, BLK]), ALU.mult).then_inc(ph.dq, 1)

            def ffn0():
                f = ff[0]

                def nf_lo(s):
                    dve.wait_ge(nf.hi, s + 1)
                    TTo(nlo, nacc, nhi, ALU.subtract).then_inc(nf.lo, 1)
                    dve.drain()

                def tq_lo(s, j):
                    e = (j + 1) % 2
                    for i, (pb, s0, ns) in enumerate(((u_ps[e], 0, 8), (u_ps[1 - e], 8, 3))):
                        dve.wait_ge(f.tq_mm, 4 * s + (2, 4)[i])
                        dve.tensor_copy(w12l[:, bass.ds(s * NT1 + s0, ns), :],
                                        pb[:, :].bitcast(F16)[:, 0:ns * P].rearrange("p (s f) -> p s f", f=P)
                                        ).then_inc(nf.tq_d, 1)

                def tile_of(t):
                    return xs[:, t * H:(t + 1) * H]

                def residual(b, last=False):
                    dve.wait_ge(f.d_mm, NT0 * (b + 1))
                    for t in range(TT):
                        TTo(tile_of(t), y_ps[t][:, :], sc_bc[:, :], ALU.mult).then_inc(f.y_rd, 1)
                    dve.drain()
                    for t in range(TT):
                        off = (b * TT + t) * H
                        xn = x_nat[:, bass.ds(off, H)] if not isinstance(b, int) else x_nat[:, off:off + H]
                        TTo(tile_of(t), tile_of(t), xn, ALU.add)
                    dve.drain()

                def body(b, first):
                    for j in range(NT0):
                        n = b * NT0 + j
                        half = j // 8
                        s = 2 * b + half
                        dve.wait_ge(f.u_mm, n + 1)
                        dve.wait_ge(f.silu, n + 1)
                        STT(out=sring[:, j % 2, :], in0=u_ps[j % 2][:, :], scalar=u_sc[:, j:j + 1],
                            in1=sring[:, j % 2, :], op0=ALU.mult, op1=ALU.mult).then_inc(f.h, 1)
                        if j == 8 or (j == 0 and not first):
                            nf_lo(s - 1)
                        if j == 1 and not first:
                            residual(b - 1)
                        if j == 2 and not first:
                            layernorm(tile_of, tile_of, f.ln)
                        k0 = sum(SHARE[8 * half:j])
                        for k in range(k0, k0 + SHARE[j]):
                            stt(nf, k, STRIPE, (k + half) % 2, s * NB + k)
                        if j == 9 and not first:
                            dve.wait_ge(f.xcp, b)
                            dve.wait_ge(f.xt_mm, 4 * b)
                        if j % 8 == 7:
                            cols = am[:, bass.ds(s * SBLK, SBLK)]
                            dequant(nf, cols, SBLK)
                        if j == 2 and not first:
                            tq_lo(2 * b - 1, j)
                        if j == 10:
                            tq_lo(2 * b, j)
                        if j == 6 and not first:
                            for kt, pb in enumerate((g_ps[1], u_ps[1], g_ps[0], u_ps[0])):
                                dve.wait_ge(f.xhi, 4 * (b - 1) + kt + 1)
                                x_lo(f, kt, pb, b - 1)
                body(0, True)
                with dve.Fori(1, B) as b:
                    body(b, False)
                nf_lo(NSTR - 1)
                residual(B - 1)
                layernorm(tile_of, tile_of, f.ln)
                tq_lo(NSTR - 1, NT0 - 1)
                for kt in range(KT):
                    dve.wait_ge(f.xhi, 4 * (B - 1) + kt + 1)
                    x_lo(f, kt, y_ps[kt], B - 1)

            def w3_quant():
                for c, (t, half, b0, nb) in enumerate(w3_part):
                    w = nb * BLK
                    for k in range(NB):
                        stt(n3, k, w, (c * NB + k) % 2, c * NB + k)
                    k0 = 8 * SBLK + t * PBLK + b0
                    dequant(n3, am[:, k0:k0 + nb], nb)
                    dve.wait_ge(n3.hi, c + 1)
                    cs = half * STRIPE
                    TTo(n3l[:, cs:cs + w], nacc[:, 0:w], n3h[:, cs:cs + w], ALU.subtract).then_inc(n3.lo, 1)
                    dve.drain()
                    if half:
                        for i in range(4 * t, 4 * t + 4):
                            _, r, s0, ns = tq3_groups[i]
                            dve.wait_ge(n3.tq_mm, 2 * i + 2)
                            dve.tensor_copy(w3l[:, s0:s0 + ns, (2 * t + r) * P:(2 * t + r + 1) * P],
                                            y_ps[(2 * i + 1) % 4][:, :].bitcast(F16)[:, 0:ns * P].rearrange(
                                                "p (s f) -> p s f", f=P)).then_inc(n3.tq_d, 1)

            def ffn1():
                f = ff[1]

                def out_view(v):
                    return v.rearrange("q (t p r) -> q t r p", t=2, r=2)

                def residual(b):
                    dve.wait_ge(f.d_mm, NT1 * (b + 1))
                    off0 = b * (TT * H)

                    def xv(t):
                        o = off0 + t * H
                        return x_nat[:, o:o + H] if isinstance(o, int) else x_nat[:, bass.ds(o, H)]
                    for t in range(TT):
                        tmp = ytmp[:, t * H:(t + 1) * H]
                        TTo(tmp, y_ps[t][:, :], sc_bc[:, :], ALU.mult).then_inc(f.y_rd, 1)
                    dve.drain()
                    for t in range(TT):
                        tmp = ytmp[:, t * H:(t + 1) * H].rearrange("q (t r p) -> q t r p", t=2, r=2)
                        TTo(out_view(xv(t)), tmp, out_view(xv(t)), ALU.add)
                    dve.drain()
                    layernorm(xv, xv, f.ln)
                    dve.drain()

                def body(b, first):
                    for j in range(NT1):
                        n = b * NT1 + j
                        dve.wait_ge(f.u_mm, n + 1)
                        dve.wait_ge(f.silu, n + 1)
                        STT(out=sring[:, j % 2, :], in0=u_ps[j % 2][:, :], scalar=u1_sc[:, j:j + 1],
                            in1=sring[:, j % 2, :], op0=ALU.mult, op1=ALU.mult).then_inc(f.h, 1)
                        if j == 1 and not first:
                            residual(b - 1)
                        if first and j == NT1 - 1:
                            w3_quant()
                body(0, True)
                with dve.Fori(1, B) as b:
                    body(b, False)
                residual(B - 1)

            dve.memset(asum3[:, :], 0.0)
            dve.wait_ge(s_const, 16 * 7)
            TTo(tmp16[:, 0:NT0], g_sc[:, :], u_sc[:, :], ALU.mult)
            dve.drain()
            dve.tensor_reduce(fac[:, 0:1], tmp16[:, 0:NT0], AX.X, ALU.max, apply_absolute_value=True
                              ).then_inc(v_init, 1)
            TS(bqs[:, 0:2], bcol[:, :, 0], SCALE, None, ALU.mult).then_inc(v_init, 1)
            dve.wait_ge(s_wraw1, 16)
            dve.tensor_reduce(fac[:, 4:5], wraw1, AX.X, ALU.max, apply_absolute_value=True).then_inc(v_init, 1)
            dve.wait_ge(p_red, 1)
            pow2_of(fac[:, 2:3], fac[:, 1:2])
            inverse_pow2(fac[:, 3:4], fac[:, 2:3], -4)
            TS(g_sc[:, :], g_sc[:, :], 1.0 / XSCALE, None, ALU.mult)
            TS(u_sc[:, :], u_sc[:, :], 1.0 / XSCALE, fac[:, 3:4], ALU.mult, ALU.mult)
            TS(sc_bc[:, :], sc_bc[:, :], fac[:, 2:3], 2.0 ** 4, ALU.mult, ALU.mult).then_inc(v_init, 1)
            dve.drain()
            attention(0)
            dve.wait_ge(p_red, 2)
            pow2_of(fac[:, 6:7], fac[:, 5:6])
            inverse_pow2(fac[:, 7:8], fac[:, 6:7], WBITS)
            dve.wait_ge(at[0].v_mm, B)
            TS(wraw1, wraw1, fac[:, 7:8], None, ALU.mult)
            dve.drain()
            dve.tensor_copy(wq_h, wraw1)
            dve.drain()
            TTo(wq_l, wraw1, wq_h, ALU.subtract)
            TS(fac[:, 6:7], fac[:, 6:7], 2.0 ** -(WBITS + XS_BITS), None, ALU.mult)
            dve.drain()
            TS(fac[:, 7:8], fac[:, 6:7], SCALE, None, ALU.mult)
            for m in range(3):
                for c in range(4):
                    absmax(m, c)
            dve.drain()
            TS(rc[:, :], am[:, :], 1e-38, None, ALU.max)
            dve.tensor_reduce(tmp16[:, 0:22], am[:, 0:176].rearrange("p (r b) -> p r b", b=8), AX.X, ALU.max)
            dve.tensor_reduce(tmp16[:, 22:24], am[:, 176:NAM].rearrange("p (r b) -> p r b", b=PBLK), AX.X, ALU.max)
            dve.drain()
            dve.reciprocal(rc[:, :], rc[:, :])
            pow2_of(rp2[:, :], tmp16[:, 0:24])
            inverse_pow2(rinvp2[:, :], rp2[:, :], WBITS)
            for c0, nr, nb in ((0, 22, 8), (176, 2, PBLK)):
                v = am[:, c0:c0 + nr * nb].rearrange("p (r b) -> p r b", b=nb)
                r0 = 0 if c0 == 0 else 22
                TTo(v, v, rinvp2[:, r0:r0 + nr].unsqueeze(2).to_broadcast([P, nr, nb]), ALU.mult)
            TTo(tmp16[:, 0:NT1], rp2[:, 0:NT1], rp2[:, NT1:2 * NT1], ALU.mult)
            dve.drain()
            dve.tensor_reduce(fac[:, 8:9], tmp16[:, 0:NT1], AX.X, ALU.max).then_inc(v_init, 1)
            ffn0()
            dve.wait_ge(p_red, 3)
            TS(fac[:, 10:11], fac[:, 9:10], TINY, None, ALU.max)
            dve.drain()
            inverse_pow2(fac[:, 11:12], fac[:, 10:11], -5)
            TS(g1_sc[:, :], rp2[:, 0:NT1], 2.0 ** -(WBITS + XS_BITS), None, ALU.mult)
            TS(u1_sc[:, :], rp2[:, NT1:2 * NT1], 2.0 ** -(WBITS + XS_BITS), fac[:, 11:12], ALU.mult, ALU.mult)
            TS(rp2[:, 22:24], rp2[:, 22:24], fac[:, 10:11], 2.0 ** (5 - WBITS), ALU.mult, ALU.mult)
            dve.drain()
            for t in range(2):
                m = TS(diag3[:, t * P:(t + 1) * P], idf[:, :], rp2[:, 22 + t:23 + t], None, ALU.mult)
            m.then_inc(v_init, 1)
            dve.wait_ge(t_misc, 3)
            src = misc_ps[:, 0:2 * P].rearrange("p (t f) -> p t f", t=2)
            dst = sc_bc[:, :].rearrange("p (t r f) -> p t r f", t=2, r=2)
            for r in range(2):
                m = dve.tensor_copy(dst[:, :, r, :], src)
            m.then_inc(v_init, 1)
            dve.memset(n3h[:, PAIR:NATW], 0.0)
            dve.memset(n3l[:, PAIR:NATW], 0.0)
            dve.drain()
            attention(1)
            ffn1()

    return nc


def kernel(**inputs):
    import numpy as _np
    import concourse.bacc as _bacc
    from concourse import mybir as _mybir
    from concourse.bass_utils import run_bass_kernel_spmd as _run

    inp = {k: _np.asarray(v) for k, v in inputs.items()}
    c = _np.ascontiguousarray
    x = inp["L0_attn_x"].reshape(B * SEQ, H)
    pad = ((0, NT1 * P - F1), (0, 0))

    def nat_tiles(w):
        t = _np.pad(w, pad).reshape(NT1, P, H).transpose(1, 0, 2).reshape(P, 4, STRIPE)
        return t.transpose(1, 0, 2)

    arrays = {
        "x_nat_in": c(x.reshape(B, TT, P, H).transpose(0, 2, 1, 3)),
        "x_T_in": c(x.reshape(B, SEQ, KT, P).transpose(0, 3, 2, 1)),
        "wqkv0_in": c(inp["L0_attn_Wqkv"].reshape(KT, P, 3 * D).transpose(1, 0, 2)),
        "wqkv1_in": c(inp["L1_attn_Wqkv"].reshape(KT, P, 3 * D).transpose(1, 0, 2).reshape(P, -1)),
        "bcol_in": c(_np.stack([inp["L0_attn_bqkv"].reshape(3, D).T, inp["L1_attn_bqkv"].reshape(3, D).T], 1)),
        "bv_in": c(_np.stack([inp["L0_attn_bqkv"][2 * D:], inp["L1_attn_bqkv"][2 * D:]])),
        "bo_in": c(_np.stack([inp["L0_attn_bo"], inp["L1_attn_bo"]])),
        "wo_in": c(_np.stack([inp["L0_attn_Wo"], inp["L1_attn_Wo"]])),
        "gsc_in": c(inp["L0_ffn_gate_scale"].reshape(NT0, P).T),
        "usc_in": c(inp["L0_ffn_up_scale"].reshape(NT0, P).T),
        "dsc_in": c(inp["L0_ffn_down_scale"].reshape(1, H)),
        "gate_T_in": c(inp["L0_ffn_gate_w"].T.reshape(KT, P, F0)),
        "up_T_in": c(inp["L0_ffn_up_w"].T.reshape(KT, P, F0)),
        "down_T_in": c(inp["L0_ffn_down_w"].T.reshape(KT, KT, P, H).transpose(0, 2, 1, 3)),
        "w12_in": c(_np.concatenate([nat_tiles(inp["L1_ffn_w1"]), nat_tiles(inp["L1_ffn_w2"])])),
        "w3_in": c(inp["L1_ffn_w3"].reshape(2, P, PAIR)),
    }
    nc = _bacc.Bacc("TRN2", target_bir_lowering=False, num_devices=1)
    ap = {n: nc.dram_tensor(n, a.shape, _mybir.dt.from_np(a.dtype), kind="ExternalInput").ap()
          for n, a in arrays.items()}
    out = nc.dram_tensor("out", (B, P, TT, H), F32, kind="ExternalOutput").ap()

    def rows(v):
        return v.unsqueeze(0).to_broadcast([P, v.shape[0]])

    io = {
        "xn": [ap["x_nat_in"][b] for b in range(B)], "xT": [ap["x_T_in"][b] for b in range(B)],
        "wqkv": [ap["wqkv0_in"]], "wqkv1": ap["wqkv1_in"], "bcol": ap["bcol_in"],
        "bv": [rows(ap["bv_in"][l]) for l in range(2)], "bo": [rows(ap["bo_in"][l]) for l in range(2)],
        "wo": [ap["wo_in"][l] for l in range(2)], "gsc": ap["gsc_in"], "usc": ap["usc_in"],
        "dsc": rows(ap["dsc_in"][0]),
        "tern": [[ap["gate_T_in"][k] for k in range(KT)], [ap["up_T_in"][k] for k in range(KT)],
                 [ap["down_T_in"][k] for k in range(KT)]],
        "w12n": ap["w12_in"], "w3n": [ap["w3_in"][t] for t in range(2)], "out": out,
    }
    build(nc, io)
    r = _run(nc, [arrays], core_ids=[0])
    got = r.results[0]["out"]
    return c(got.transpose(0, 2, 1, 3)).reshape(B, SEQ, H)
```

```python
from contextlib import ExitStack

import numpy as np
import concourse.bass as bass
from concourse import mybir

F32 = mybir.dt.float32
F16 = mybir.dt.float16
BF16 = mybir.dt.bfloat16
F8 = mybir.dt.float8e4
I32 = mybir.dt.int32
ALU = mybir.AluOpType
ACT = mybir.ActivationFunctionType
AX = mybir.AxisListType
RMAX = bass.bass_isa.ReduceOp.max

P = 128
B, SEQ, H = 4, 512, 512
D = H // 4
KT = H // P
TT = SEQ // P
F0 = 2048
NT0 = F0 // P
F1 = 1376
NT1 = -(-F1 // P)
LASTROWS = F1 - (NT1 - 1) * P
SCALE = float(D) ** -0.5
EPS = 1e-5
BLK = 64
STRIPE = NT1 * P
SBLK = STRIPE // BLK
NSTR = 2 * KT * NT1 * P // STRIPE
PAIR = 2 * F1
PBLK = PAIR // BLK
NATW = 2 * F1 + 32
XS_BITS = 11
XSCALE = 2.0 ** XS_BITS
WBITS = 13
TINY = 2.0 ** -60

NF4 = np.array([-1.0, -0.6961928009986877, -0.5250730514526367, -0.39491748809814453,
                -0.28444138169288635, -0.18477343022823334, -0.09105003625154495, 0.0,
                0.07958029955625534, 0.16093020141124725, 0.24611230194568634,
                0.33791524171829224, 0.44070982933044434, 0.5626170039176941,
                0.7229568362236023, 1.0], np.float32)
BOUNDS = (NF4[:-1] + NF4[1:]) * np.float32(0.5)
STEPS = NF4[1:] - NF4[:-1]
NB = len(BOUNDS)
BIG = 2.0 ** 60


SHARE_0 = [0, 0, 0, 0, 0, 3, 3, 5, 4]
SHARE = [[0, 2, 2, 1, 2, 1, 1, 3, 3, 0, 0, 0, 0, 0, 0, 0], [0, 0, 0, 0, 0, 0, 0, 0, 0, 0, 1, 2, 3, 3, 2, 4]]
AHEAD = KT
SPLIT = 9
SHARE_A = [(0, 0, 0), (1, 3, 1), (1, 3, 2), (1, 3, 0)]
SHARE_F = [[0, 1, 3, 3, 4, 3, 1, 0, 0, 0, 0], [0, 0, 0, 0, 0, 0, 0, 3, 3, 3, 3]]


def relus_by(share, j):
    n = sum(share[:j + 1])
    return min(NB, n + 1) if n else 0


def ring_used(b, j):
    return j >= 2 or not isinstance(b, int) or b > 0


def build(nc, io):
    ctx = ExitStack()
    with ctx:
        def sb(name, shape, dt=F32):
            return ctx.enter_context(nc.sbuf_tensor(name, shape, dt))

        def sem(name):
            return ctx.enter_context(nc.semaphore(name))

        def wait(eng, s, n):
            if not isinstance(n, int) or n > 0:
                eng.wait_ge(s, n)

        x_nat = sb("x_nat", [P, B * TT * H])
        xh = sb("xh", [P, KT, B * SEQ], F16)
        xl = sb("xl", [P, KT, B * SEQ], F16)
        reg_t = sb("reg_t", [P, 12288])
        reg_a = sb("reg_a", [P, 11264])
        reg_n = sb("reg_n", [P, 5632 + 2048])
        sring = sb("sring", [P, 2, SEQ])
        wqkv = sb("wqkv", [P, 1536])
        wo = sb("wo", [P, H])
        bo_bc = sb("bo_bc", [P, H])
        sc_bc = sb("sc_bc", [P, H])
        bv_bc = sb("bv_bc", [P, 2, D])
        idf = sb("idf", [P, P])
        idh = sb("idh", [P, P], F16)
        ones = sb("ones", [P, P])
        bcol = sb("bcol", [P, 2, 3])
        bqs = sb("bqs", [P, 2])
        g_sc = sb("g_sc", [P, NT0])
        u_sc = sb("u_sc", [P, NT0])
        g1_sc = sb("g1_sc", [P, NT1])
        u1_sc = sb("u1_sc", [P, NT1])
        tmp16 = sb("tmp16", [P, 26])
        asum = sb("asum", [P, 12])
        asum3 = sb("asum3", [P, 3])
        thr = sb("thr", [P, 3, 2])
        nmax = sb("nmax", [P, TT])
        rsum = sb("rsum", [P, TT])
        rinv = sb("rinv", [P, TT])
        stats = sb("stats", [P, TT, 6])
        mv = sb("mv", [P, TT, 2])
        nv = sb("nv", [P, 4, TT])
        NAM = 2 * KT * NT1 * 2 + 2 * PBLK
        am = sb("am", [P, NAM])
        rc = sb("rc", [P, NAM])
        rp2 = sb("rp2", [P, 24])
        rinvp2 = sb("rinvp2", [P, 24])
        fac = sb("fac", [P, 12])

        def view(reg, lo, words, dt=F32):
            v = reg[:, lo:lo + words]
            return v if dt == F32 else v.bitcast(dt)

        tg = view(reg_t, 0, 4096, F16).rearrange("p (k f) -> p k f", k=KT)
        tu = view(reg_t, 4096, 4096, F16).rearrange("p (k f) -> p k f", k=KT)
        td = view(reg_t, 8192, 2048, F8).rearrange("p (k f) -> p k f", k=NT0)
        xs = view(reg_t, 10240, 2048)
        below = [view(reg_t, 10240 + 1024 * i, 1024, BF16) for i in range(2)]
        w3h = view(reg_t, 0, 2816, F16).rearrange("p (k f) -> p k f", k=NT1)
        w3l = view(reg_t, 2816, 2816, F16).rearrange("p (k f) -> p k f", k=NT1)
        hh1 = view(reg_t, 5632, 2816, F16).rearrange("p (k f) -> p k f", k=NT1)
        hl1 = view(reg_t, 8448, 2816, F16).rearrange("p (k f) -> p k f", k=NT1)
        w12h = view(reg_a, 0, 5632, F16).rearrange("p (s f) -> p s f", f=P)
        w12l = view(reg_a, 5632, 5632, F16).rearrange("p (s f) -> p s f", f=P)
        xT = [view(reg_a, 6144 + 2048 * i, 2048).rearrange("p (k f) -> p k f", k=KT) for i in range(2)]
        wraw1 = view(reg_a, 9728, 1536)
        raw = [view(reg_n, 2048 * i, 2048) for i in range(3)]
        nraw = view(reg_n, 0, STRIPE)
        nacc = view(reg_n, 1408, STRIPE)
        nrel = [view(reg_n, 2816 + 704 * i, 704, BF16) for i in range(2)]
        nhi = view(reg_n, 4224, 704, F16)
        nlo = view(reg_n, 4928, 704, F16)
        n3h = view(reg_n, 4224, NATW // 2, F16)
        n3l = view(reg_n, 4224 + NATW // 2, NATW // 2, F16)
        hring = view(reg_n, 5632, 1024, F16).rearrange("p (s f) -> p s f", s=4)
        lring = view(reg_n, 6656, 1024, F16).rearrange("p (s f) -> p s f", s=4)
        wq_h = view(wqkv, 0, 768, F16)
        wq_l = view(wqkv, 768, 768, F16)

        def attn_bufs(reg, at):
            return dict(qT=view(reg, at, 512), kT=view(reg, at + 512, 512), v=view(reg, at + 1024, 512),
                        oT=view(reg, at + 1536, 512),
                        pr=view(reg, at + 2048, 2048).rearrange("p (t k) -> p t k", t=TT),
                        pT=view(reg, at + 4096, 2048).rearrange("p (t q) -> p t q", t=TT))

        diag3 = view(reg_t, 11776, 2 * P)
        nraw3 = [nraw, wqkv[:, 0:STRIPE]]
        am3 = [nraw, view(reg_n, 2816, STRIPE)]
        ytmp = view(reg_n, 0, TT * H)
        tq3_groups = [(t, r, s0, ns) for t in range(2) for r in range(2) for s0, ns in ((0, 8), (8, NT1 - 8))]

        bufs = [attn_bufs(reg_a, 0), attn_bufs(reg_t, 5632)]

        def hidden1(b, j):
            if isinstance(b, int) and b == 1 and j < AHEAD:
                return xh[:, j, 0:SEQ], xl[:, j, 0:SEQ]
            return hh1[:, j, :], hl1[:, j, :]

        def tq3_bank(i, part):
            return ((y_ps, bank[0:4])[i // 4])[(2 * i + part) % 4]

        bank = [ctx.enter_context(nc.psum_tensor(f"bank{i}", [P, 512], F32)) for i in range(8)]
        bank16 = [t[:, :].bitcast(F16) for t in bank]
        q_ps, k_ps, v_ps, o_ps = bank[0], bank[1], bank[2], bank[3]
        roll = bank[4:8]
        g_ps, u_ps = bank[0:2], bank[2:4]
        y_ps = bank[4:8]
        misc_ps = bank[3]

        s_const = sem("s_const")
        s_w0 = sem("s_w0")
        s_wq0 = [sem(f"s_wq0{k}") for k in range(KT)]
        s_xT0 = [sem(f"s_xTk{k}") for k in range(KT)]
        s_xT = [sem("s_xT0"), sem("s_xT1")]
        s_xn = [sem(f"s_xn{i}") for i in range(B)]
        s_raw = [sem(f"s_raw{i}") for i in range(3)]
        s_wraw1 = sem("s_wraw1")
        s_w1 = sem("s_w1")
        s_nraw = sem("s_nraw")
        s_raw3 = [sem("s_raw30"), sem("s_raw31")]
        s_out = sem("s_out")
        p_init = sem("p_init")
        p_red = sem("p_red")
        a_sum = sem("a_sum")
        a_neg = sem("a_neg")
        v_tern = sem("v_tern")
        v_wmax = sem("v_wmax")
        v_raw = sem("v_raw")
        s_am3 = [sem("s_am30"), sem("s_am31")]
        v_am3 = sem("v_am3")
        v_rc = sem("v_rc")
        v_diag = sem("v_diag")
        v_sc1 = sem("v_sc1")
        v_init = sem("v_init")
        t_misc = sem("t_misc")
        v_misc = sem("v_misc")

        class AttnSems:

            def __init__(self, tag):
                self.q_mm = sem(tag + "_q_mm")
                self.k_mm = sem(tag + "_k_mm")
                self.v_mm = sem(tag + "_v_mm")
                self.s_mm = sem(tag + "_s_mm")
                self.t_mm = sem(tag + "_t_mm")
                self.o_mm = sem(tag + "_o_mm")
                self.y_mm = sem(tag + "_y_mm")
                self.xt_mm = sem(tag + "_xt_mm")
                self.q_sb = sem(tag + "_q_sb")
                self.k_sb = sem(tag + "_k_sb")
                self.v_sb = sem(tag + "_v_sb")
                self.mx = sem(tag + "_mx")
                self.exp = sem(tag + "_exp")
                self.pt_a = sem(tag + "_pt_a")
                self.pt_d = sem(tag + "_pt_d")
                self.o_sb = sem(tag + "_o_sb")
                self.xb = sem(tag + "_xb")
                self.y_rd = sem(tag + "_y_rd")
                self.ln = sem(tag + "_ln")
                self.xhi = sem(tag + "_xhi")
                self.xlo = sem(tag + "_xlo")

        class FfnSems:

            def __init__(self, tag):
                self.g_mm = sem(tag + "_g_mm")
                self.u_mm = sem(tag + "_u_mm")
                self.d_mm = sem(tag + "_d_mm")
                self.xt_mm = sem(tag + "_xt_mm")
                self.tq_mm = sem(tag + "_tq_mm")
                self.silu = sem(tag + "_silu")
                self.h = sem(tag + "_h")
                self.hi = sem(tag + "_hi")
                self.lo = sem(tag + "_lo")
                self.y_rd = sem(tag + "_y_rd")
                self.ln = sem(tag + "_ln")
                self.xb = sem(tag + "_xb")
                self.xcp = sem(tag + "_xcp")
                self.xhi = sem(tag + "_xhi")
                self.xlo = sem(tag + "_xlo")

        class QuantSems:

            def __init__(self, tag):
                self.xn = sem(tag + "_xn")
                self.rel = sem(tag + "_rel")
                self.stt = sem(tag + "_stt")
                self.dq = sem(tag + "_dq")
                self.hi = sem(tag + "_hi")
                self.lo = sem(tag + "_lo")
                self.tq_mm = sem(tag + "_tq_mm")
                self.tq_a = sem(tag + "_tq_a")
                self.dqp = sem(tag + "_dqp")
                self.lop = sem(tag + "_lop")
                self.tq_d = sem(tag + "_tq_d")

        at = [AttnSems(f"a{l}") for l in range(2)]
        ff = [FfnSems(f"f{l}") for l in range(2)]
        nf = QuantSems("nf")
        n3 = QuantSems("n3")

        stream = ([("sum", m, c) for m in range(3) for c in range(4)]
                  + [("tern", 0, c) for c in range(4)] + [("amax", 0, c) for c in range(2)]
                  + [("tern", 1, c) for c in range(4)] + [("amax", 0, 2), ("amax", 0, 3), ("amax", 1, 0)]
                  + [("tern", 2, c) for c in range(4)] + [("amax", 1, c) for c in range(1, 4)])

        LOAD_X = (2, 11, 14, 18)
        BY_ACT = 10
        n_three = len(stream) - 5
        slot_of = [n % 3 if n < n_three else (n - n_three) % 2 for n in range(len(stream))]

        def chunk_used(n):
            return {"sum": a_sum, "tern": v_tern, "amax": v_raw}[stream[n][0]]

        def used_count(n):
            return sum(stream[i][0] == stream[n][0] for i in range(n + 1))
        w3_part = [(t, half, half * SBLK, SBLK if half == 0 else PBLK - SBLK) for t in range(2) for half in range(2)]

        def chunk_src(kind, m, c):
            if kind == "amax":
                return io["w12n"][4 * m + c], STRIPE
            return io["tern"][m][c], 2048

        def tern_dst(m, c):
            return (tg, tu)[m][:, c, :] if m < 2 else td[:, 4 * c:4 * c + 4, :].rearrange("p k f -> p (k f)")

        def tern_mode(m):
            return {"saturate": False} if m == 2 else {}

        def chunk_wait(eng, n):
            eng.wait_ge(s_raw[slot_of[n]], 16 * slot_of[:n + 1].count(slot_of[n]))

        block = ctx.enter_context(nc.Block())

        @block.sync
        def _(sp):
            for kt in range(KT):
                sp.dma_start(wqkv[:, kt * 3 * D:(kt + 1) * 3 * D], io["wqkv"][0][:, kt, :]).then_inc(s_wq0[kt], 16)
            sp.dma_start(bcol[:, :, :], io["bcol"]).then_inc(s_const, 16)
            sp.dma_start(bv_bc[:, 0, :], io["bv"][0]).then_inc(s_const, 16)
            sp.dma_start(bv_bc[:, 1, :], io["bv"][1]).then_inc(s_const, 16)
            sp.dma_start(bo_bc[:, :], io["bo"][0]).then_inc(s_const, 16)
            sp.dma_start(wo[:, :], io["wo"][0]).then_inc(s_w0, 16)
            sp.dma_start(g_sc[:, :], io["gsc"]).then_inc(s_const, 16)
            sp.dma_start(u_sc[:, :], io["usc"]).then_inc(s_const, 16)
            sp.dma_start(sc_bc[:, :], io["dsc"]).then_inc(s_const, 16)

            def load_x(b):
                sp.dma_start(x_nat[:, b * TT * H:(b + 1) * TT * H].rearrange("p (t f) -> p t f", t=TT),
                             io["xn"][b]).then_inc(s_xn[b], 16)

            for n, (kind, m, c) in enumerate(stream):
                before = [i for i in range(n) if slot_of[i] == slot_of[n]]
                if before:
                    sp.wait_ge(chunk_used(before[-1]), used_count(before[-1]))
                src, w = chunk_src(kind, m, c)
                dst = raw[slot_of[n]][:, 0:w]
                if len(src.shape) == 3:
                    dst = dst.rearrange("p (k f) -> p k f", k=src.shape[1])
                sp.dma_start(dst, src).then_inc(s_raw[slot_of[n]], 16)
                if n in LOAD_X:
                    load_x(LOAD_X.index(n))
            sp.wait_ge(at[0].v_mm, B)
            sp.dma_start(wraw1, io["wqkv1"]).then_inc(s_wraw1, 16)
            sp.wait_ge(at[0].y_mm, B * TT)
            sp.dma_start(wo[:, :], io["wo"][1]).then_inc(s_w1, 16)
            sp.wait_ge(at[0].xb, B * TT)
            sp.dma_start(bo_bc[:, :], io["bo"][1]).then_inc(s_w1, 16)

            def load_stripe(s):
                src = io["w12n"][s] if isinstance(s, int) else \
                    io["w12n"][bass.ds(s, 1), :, :].rearrange("a p f -> p (a f)")
                sp.dma_start(nraw, src).then_inc(s_nraw, 16)

            def copy_x(b):
                sp.wait_ge(ff[0].ln, b + 1)
                o = b * (TT * H)
                dst = x_nat[:, o:o + TT * H] if isinstance(b, int) else x_nat[:, bass.ds(o, TT * H)]
                sp.dma_start(dst, xs).then_inc(ff[0].xcp, 16)

            n_last = len(stream) - 1
            sp.wait_ge(v_raw, used_count(n_last))
            load_stripe(0)
            sp.wait_ge(nf.rel, NB)
            load_stripe(1)
            with sp.Fori(1, B) as b:
                sp.wait_ge(nf.rel, b * (2 * NB))
                load_stripe(b * 2)
                copy_x(b - 1)
                sp.wait_ge(nf.rel, b * (2 * NB) + NB)
                load_stripe(b * 2 + 1)

            def load_w3(c, dst, done):
                t, _, b0, nb = w3_part[c]
                sp.dma_start(dst[:, 0:nb * BLK], io["w3n"][t][:, b0 * BLK:(b0 + nb) * BLK]).then_inc(done, 16)

            sp.wait_ge(nf.rel, NSTR * NB)
            load_w3(2, am3[0], s_am3[0])
            sp.wait_ge(nf.dq, NSTR)
            load_w3(1, am3[1], s_am3[1])
            copy_x(B - 1)
            sp.wait_ge(v_am3, 2)
            load_w3(3, am3[1], s_am3[1])
            load_w3(0, am3[0], s_am3[0])
            for c in range(1, len(w3_part)):
                if c == 1:
                    sp.wait_ge(at[1].v_mm, B)
                else:
                    sp.wait_ge(n3.rel, (c - 1) * NB)
                load_w3(c, nraw3[c % 2], s_raw3[c % 2])
            with sp.Fori(0, B) as b:
                for t in range(TT):
                    sp.wait_ge(ff[1].ln, b * TT + (t + 1))
                    sp.dma_start(io["out"][bass.ds(b, 1), :, t, :].rearrange("a p f -> p (a f)"),
                                 x_nat[:, bass.ds(b * (TT * H) + t * H, H)]).then_inc(s_out, 16)
            sp.wait_ge(s_out, 16 * B * TT)

        @block.gpsimd
        def _(pool):
            pool.memset(idf[:, :], 0.0).then_inc(p_init, 1)
            pool.memset(ones[:, :], 1.0).then_inc(p_init, 1)
            pool.wait_ge(p_init, 2)
            pool.affine_select(out=idf[:, :], in_=idf[:, :], compare_op=ALU.not_equal, fill=1.0, base=0,
                               pattern=[[-1, P]], channel_multiplier=1).then_inc(p_init, 1)
            pool.wait_ge(p_init, 3)
            pool.tensor_copy(idh[:, :], idf[:, :]).then_inc(p_init, 1)
            pool.wait_ge(v_init, 1)
            pool.partition_all_reduce(fac[:, 1:2], fac[:, 0:1], P, RMAX).then_inc(p_red, 1)
            def add_bo(l, b):
                a = at[l]
                for t in range(TT):
                    v = x_nat[:, (b * TT + t) * H:(b * TT + t + 1) * H]
                    pool.tensor_tensor(v, v, bo_bc[:, :], ALU.add).then_inc(a.xb, 1)

            pool.wait_ge(s_const, 16 * 7)
            for b in range(B):
                pool.wait_ge(s_xn[b], 16)
                add_bo(0, b)

            def lo0(n, j):
                f = ff[0]
                pool.wait_ge(f.hi, n + 1)
                pool.tensor_tensor(lring[:, j % 4, :], sring[:, j % 2, :], hring[:, j % 4, :],
                                   ALU.subtract).then_inc(f.lo, 1)

            def norm_stripe(s):
                pool.wait_ge(s_nraw, 16 * (s + 1))
                v = nraw.rearrange("p (b c) -> p b c", c=BLK)
                r = rc[:, bass.ds(s * SBLK, SBLK)].unsqueeze(2).to_broadcast([P, SBLK, BLK])
                pool.tensor_tensor(v, v, r, ALU.mult).then_inc(nf.xn, 1)

            def add_x(b):
                f = ff[0]
                pool.wait_ge(f.y_rd, 4 * b + 4)
                for t in range(TT):
                    off = (b * TT + t) * H
                    xn = x_nat[:, bass.ds(off, H)] if not isinstance(b, int) else x_nat[:, off:off + H]
                    tile = xs[:, t * H:(t + 1) * H]
                    m = pool.tensor_tensor(tile, tile, xn, ALU.add)
                m.then_inc(f.xb, 1)

            def body(b, first):
                for j in range(NT0):
                    lo0(b * NT0 + j, j)
                    if j == (3 if first else 0):
                        if first:
                            pool.wait_ge(v_rc, 1)
                        norm_stripe(2 * b)
                    if j == SPLIT:
                        norm_stripe(2 * b + 1)
                    if j == 6 and first:
                        pool.wait_ge(v_wmax, 1)
                        pool.partition_all_reduce(fac[:, 5:6], fac[:, 4:5], P, RMAX).then_inc(p_red, 1)
                    if j == 1 and not first:
                        add_x(b - 1)
            body(0, True)
            with pool.Fori(1, B) as b:
                body(b, False)
            add_x(B - 1)

            pool.wait_ge(v_init, 4)
            pool.partition_all_reduce(fac[:, 9:10], fac[:, 8:9], P, RMAX).then_inc(p_red, 1)

            def norm_w3(c):
                t, half, b0, nb = w3_part[c]
                if c == 0:
                    pool.wait_ge(v_rc, 2)
                else:
                    pool.wait_ge(s_raw3[c % 2], 16 * ((c + 1) // 2))
                v = nraw3[c % 2][:, 0:nb * BLK].rearrange("p (b c) -> p b c", c=BLK)
                k0 = 8 * SBLK + t * PBLK + b0
                r = rc[:, k0:k0 + nb].unsqueeze(2).to_broadcast([P, nb, BLK])
                pool.tensor_tensor(v, v, r, ALU.mult).then_inc(n3.xn, 1)

            pool.wait_ge(s_w1, 32)
            for b in range(B):
                pool.wait_ge(ff[0].xcp, 16 * (b + 1))
                pool.wait_ge(ff[0].xlo, 4 * (b + 1))
                add_bo(1, b)
                if b == 0:
                    norm_w3(0)
                if b == B - 1:
                    norm_w3(1)
                    w = w3_part[0][3] * BLK
                    pool.wait_ge(n3.stt, NB)
                    v = nacc[:, 0:w].rearrange("p (b c) -> p b c", c=BLK)
                    scales = am[:, 8 * SBLK:8 * SBLK + w3_part[0][3]]
                    pool.tensor_tensor(v, v, scales.unsqueeze(2).to_broadcast([P, w3_part[0][3], BLK]),
                                       ALU.mult).then_inc(n3.dqp, 1)
                    pool.wait_ge(n3.hi, 1)
                    pool.tensor_tensor(n3l[:, 0:w], nacc[:, 0:w], n3h[:, 0:w], ALU.subtract).then_inc(n3.lop, 1)

            def lo1(b, j):
                n = b * NT1 + j
                hi, lo = hidden1(b, j)
                pool.wait_ge(ff[1].hi, n + 1)
                pool.tensor_tensor(lo, sring[:, j % 2, :], hi, ALU.subtract).then_inc(ff[1].lo, 1)

            for j in range(NT1):
                lo1(0, j)
                if j == 2:
                    norm_w3(2)
                if j == 8:
                    norm_w3(3)
            for j in range(NT1):
                lo1(1, j)
            with pool.Fori(2, B) as b:
                for j in range(NT1):
                    lo1(b, j)

        @block.scalar
        def _(act):
            def load_xT(b):
                act.dma_start(xT[b % 2], io["xT"][b]).then_inc(s_xT[b % 2], 16)

            for kt in range(KT):
                act.dma_start(xT[0][:, kt, :], io["xT"][0][:, kt, :]).then_inc(s_xT0[kt], 16)
            load_xT(1)
            act.wait_ge(v_init, 2)

            def sum_abs(n0, n1):
                for n in range(n0, n1):
                    chunk_wait(act, n)
                    act.activation(raw[slot_of[n]], raw[slot_of[n]], ACT.Abs,
                                   accum_out=asum[:, n:n + 1]).then_inc(a_sum, 1)

            def compare(m, c):
                n = stream.index(("tern", m, c))
                chunk_wait(act, n)
                act.wait_ge(v_misc, 2)
                i = 4 * m + c
                wait(act, v_tern, i - 1)
                act.activation(below[i % 2], raw[slot_of[n]], ACT.Relu, scale=BIG, bias=thr[:, m, 1:2])
                act.drain()
                act.activation(below[i % 2], below[i % 2], ACT.Exp, scale=-BIG).then_inc(a_neg, 1)

            def q_evac(l, b):
                a, u = at[l], bufs[l]
                act.wait_ge(a.q_mm, b + 1)
                sc = SCALE if l == 0 else fac[:, 7:8]
                act.activation(u["qT"], q_ps[:, :], ACT.Identity, bias=bqs[:, l:l + 1], scale=sc).then_inc(a.q_sb, 1)

            def x_hi(a, kt, src, b):
                act.activation(xh[:, kt, bass.ds(b * SEQ, SEQ)] if not isinstance(b, int) else
                               xh[:, kt, b * SEQ:(b + 1) * SEQ], src[:, :], ACT.Copy, scale=XSCALE).then_inc(a.xhi, 1)

            def attention(l):
                a, u = at[l], bufs[l]
                q_evac(l, 0)
                if l == 0:
                    sum_abs(0, 3)
                for b in range(B):
                    for t in range(TT):
                        act.wait_ge(a.mx, 4 * b + t + 1)
                        wait(act, a.t_mm, 4 * b)
                        act.activation(u["pr"][:, t, :], roll[t][:, :], ACT.Exp, bias=nmax[:, t:t + 1],
                                       accum_out=rsum[:, t:t + 1]).then_inc(a.exp, 1)
                    if b + 1 < B:
                        q_evac(l, b + 1)
                    if l == 0 and b == 0:
                        sum_abs(3, 6)
                    if l == 0 and b >= 1:
                        compare(b - 1, 0)
                    if l == 1:
                        relu_a(b, 0)
                    if l == 1 and b == 0:
                        act.wait_ge(ff[0].xcp, 16 * B)
                    for kt in (0, 2):
                        act.wait_ge(a.t_mm, 4 * b + kt + 1)
                        act.activation(u["pT"][:, kt, :], roll[kt][:, :], ACT.Copy).then_inc(a.pt_a, 1)
                    if l == 0 and b + 2 < B:
                        act.wait_ge(a.v_mm, b + 1)
                        load_xT(b + 2)
                    if l == 1:
                        relu_a(b, 1)
                    if l == 0 and b >= 1:
                        compare(b - 1, 1)
                    act.wait_ge(a.o_mm, b + 1)
                    act.activation(u["oT"], o_ps[:, :], ACT.Copy).then_inc(a.o_sb, 1)
                    if b >= 1:
                        for kt in range(KT):
                            act.wait_ge(a.xt_mm, 4 * (b - 1) + kt + 1)
                            x_hi(a, kt, roll[kt], b - 1)
                    elif l == 1:
                        last_x_hi(ff[0])
                    if l == 0 and b == 0:
                        sum_abs(6, 12)
                    if l == 0 and b >= 1:
                        for c in range(2, 4 if b < B - 1 else 2):
                            compare(b - 1, c)
                    if l == 1:
                        relu_a(b, 2)
            def last_x_hi(a):
                for kt in range(KT):
                    act.wait_ge(a.xt_mm, 4 * (B - 1) + kt + 1)
                    x_hi(a, kt, roll[kt], B - 1)

            def relus_w3(c, k0, n):
                w = w3_part[c][3] * BLK
                for k in range(k0, k0 + n):
                    if k == 0:
                        act.wait_ge(n3.xn, c + 1)
                    m = c * NB + k
                    if m >= 2:
                        act.wait_ge(n3.stt, m - 1)
                    act.activation(nrel[m % 2][:, 0:w], nraw3[c % 2][:, 0:w], ACT.Relu, scale=BIG,
                                   bias=-BIG * float(BOUNDS[k])).then_inc(n3.rel, 1)

            def relu_a(b, i):
                k0 = sum(sum(p) for p in SHARE_A[:b]) + sum(SHARE_A[b][:i])
                relus_w3(0, k0, SHARE_A[b][i])

            def w3_hi(c):
                t, half, b0, nb = w3_part[c]
                w = nb * BLK
                if c == 0:
                    act.wait_ge(n3.dqp, 1)
                else:
                    act.wait_ge(n3.dq, c)
                if half == 0:
                    wait(act, n3.tq_mm, 8 * t)
                act.activation(n3h[:, half * STRIPE:half * STRIPE + w], nacc[:, 0:w], ACT.Copy).then_inc(n3.hi, 1)

            def w3_tq_hi(i):
                t, r, s0, ns = tq3_groups[i]
                act.wait_ge(n3.tq_mm, 2 * i + 1)
                act.activation(w3h[:, s0:s0 + ns, (2 * t + r) * P:(2 * t + r + 1) * P],
                               tq3_bank(i, 0)[:, :].bitcast(F16)[:, 0:ns * P].rearrange(
                                   "p (s f) -> p s f", f=P), ACT.Copy).then_inc(n3.tq_a, 1)

            def ffn0():
                f = ff[0]

                def tq_hi(s, j):
                    e = (j + 1) % 2
                    for i, (pb, s0, ns) in enumerate(((g_ps[e], 0, 8), (g_ps[1 - e], 8, 3))):
                        act.wait_ge(f.tq_mm, 4 * s + (1, 3)[i])
                        act.activation(w12h[:, bass.ds(s * NT1 + s0, ns), :],
                                       pb[:, :].bitcast(F16)[:, 0:ns * P].rearrange("p (s f) -> p s f", f=P),
                                       ACT.Copy).then_inc(nf.tq_a, 1)

                def body(b, first):
                    for j in range(NT0):
                        n = b * NT0 + j
                        half = int(j >= SPLIT)
                        s = 2 * b + half
                        act.wait_ge(f.g_mm, n + 1)
                        wait(act, f.lo, n - 1 if not first or j >= 2 else 0)
                        act.activation(sring[:, j % 2, :], g_ps[j % 2][:, :], ACT.Silu,
                                       scale=g_sc[:, j:j + 1]).then_inc(f.silu, 1)
                        if first and j == 3:
                            last_x_hi(at[0])
                        share = SHARE_0 if first and half == 0 else SHARE[half]
                        for k in range(sum(share[:j]), sum(share[:j + 1])):
                            if k == 0:
                                act.wait_ge(nf.xn, s + 1)
                            m = s * NB + k
                            if not (first and half == 0 and k < 2):
                                act.wait_ge(nf.stt, m - 1)
                            act.activation(nrel[(k + half) % 2], nraw, ACT.Relu, scale=BIG,
                                           bias=-BIG * float(BOUNDS[k])).then_inc(nf.rel, 1)
                        act.wait_ge(f.h, n + 1)
                        wait(act, f.d_mm, n - 3 if not first or j >= 4 else 0)
                        act.activation(hring[:, j % 4, :], sring[:, j % 2, :], ACT.Copy).then_inc(f.hi, 1)
                        if j == SPLIT or (j == 0 and not first):
                            sd = s - 1
                            act.wait_ge(nf.dq, sd + 1)
                            wait(act, f.tq_mm, 4 * sd if not (first and j == SPLIT) else 0)
                            act.activation(nhi, nacc, ACT.Copy).then_inc(nf.hi, 1)
                        if j == 2 and not first:
                            tq_hi(2 * b - 1, j)
                        if j == SPLIT + 2:
                            tq_hi(2 * b, j)
                        if j == 6 and not first:
                            for kt, pb in enumerate((g_ps[1], u_ps[1], g_ps[0], u_ps[0])):
                                act.wait_ge(f.xt_mm, 4 * (b - 1) + kt + 1)
                                x_hi(f, kt, pb, b - 1)
                body(0, True)
                with act.Fori(1, B) as b:
                    body(b, False)
                act.wait_ge(nf.dq, NSTR)
                act.wait_ge(f.tq_mm, 4 * (NSTR - 1))
                act.activation(nhi, nacc, ACT.Copy).then_inc(nf.hi, 1)
                tq_hi(NSTR - 1, NT0 - 1)

            def ffn1():
                f = ff[1]

                def silu(b, j):
                    n = b * NT1 + j
                    act.wait_ge(f.g_mm, n + 1)
                    if ring_used(b, j):
                        act.wait_ge(f.lo, n - 1 if j else n)
                    act.activation(sring[:, j % 2, :], g_ps[j % 2][:, :], ACT.Silu,
                                   scale=g1_sc[:, j:j + 1]).then_inc(f.silu, 1)

                def hi(b, j):
                    act.wait_ge(f.h, b * NT1 + j + 1)
                    act.activation(hidden1(b, j)[0], sring[:, j % 2, :], ACT.Copy).then_inc(f.hi, 1)

                for j in range(NT1):
                    silu(0, j)
                    if j == 3:
                        last_x_hi(at[1])
                    hi(0, j)
                    if j in (0, 7):
                        w3_hi(j // 7)
                    for c in (1, 2):
                        k0, k1 = relus_by(SHARE_F[c - 1], j - 1), relus_by(SHARE_F[c - 1], j)
                        relus_w3(c, k0, k1 - k0)
                w3_tq_hi(0)
                w3_tq_hi(1)
                for j in range(AHEAD):
                    silu(1, j)
                    hi(1, j)
                    if j == 0:
                        w3_tq_hi(2)
                        w3_tq_hi(3)
                        k0 = relus_by(SHARE_F[1], NT1 - 1)
                        relus_w3(2, k0, NB - k0)
                    if j == 1:
                        w3_hi(2)
                    if j == 2:
                        relus_w3(3, 0, 3)
                relus_w3(3, 3, NB - 3)
                w3_hi(3)
                for i in range(4, 8):
                    w3_tq_hi(i)
                for j in range(AHEAD, NT1):
                    silu(1, j)
                    hi(1, j)
                with act.Fori(2, B) as b:
                    for j in range(NT1):
                        silu(b, j)
                        hi(b, j)

            attention(0)
            ffn0()
            attention(1)
            ffn1()

        @block.tensor
        def _(pe):
            def operands(l, b):
                if l == 0:
                    return [(wqkv[:, :].rearrange("p (k f) -> p k f", k=KT), xT[b % 2], 0)]
                wh = wq_h.rearrange("p (k f) -> p k f", k=KT)
                wl = wq_l.rearrange("p (k f) -> p k f", k=KT)
                return [(wh, xh, b * SEQ), (wh, xl, b * SEQ), (wl, xh, b * SEQ)]

            def project_qk(l, b):
                a = at[l]
                if l == 0:
                    if b:
                        pe.wait_ge(s_xT[b % 2], 16 * ((b + 1) // 2))
                else:
                    pe.wait_ge(ff[0].xlo, 4 * (b + 1))
                passes = operands(l, b)
                np_ = KT * len(passes)
                for part, (ps, mm, used) in enumerate(((q_ps, a.q_mm, a.q_sb), (k_ps, a.k_mm, a.k_sb))):
                    wait(pe, used, b)
                    i = 0
                    for kt in range(KT):
                        if l == 0 and b == 0 and part == 0:
                            pe.wait_ge(s_xT0[kt], 16)
                            pe.wait_ge(s_wq0[kt], 16)
                        for w, x, c0 in passes:
                            m = pe.matmul(ps[:, :], w[:, kt, part * D:(part + 1) * D], x[:, kt, c0:c0 + SEQ],
                                          start=(i == 0), stop=(i == np_ - 1))
                            i += 1
                    m.then_inc(mm, 1)

            def project_v(l, b):
                a = at[l]
                passes = operands(l, b)
                np_ = KT * len(passes)
                wait(pe, a.v_sb, b)
                for t in range(TT):
                    i = 0
                    for kt in range(KT):
                        for w, x, c0 in passes:
                            m = pe.matmul(v_ps[:, t * D:(t + 1) * D], x[:, kt, c0 + t * P:c0 + (t + 1) * P],
                                          w[:, kt, 2 * D:3 * D], start=(i == 0), stop=(i == np_ - 1))
                            i += 1
                m.then_inc(a.v_mm, 1)

            def transpose_x(src, done, banks, kts):
                for kt in kts:
                    for t in range(TT):
                        m = pe.transpose(banks[kt][:, t * P:(t + 1) * P], src[:, t * H + kt * P:t * H + (kt + 1) * P],
                                         idf[:, :])
                    m.then_inc(done, 1)

            def attention(l):
                a, u = at[l], bufs[l]
                project_qk(l, 0)
                project_v(l, 0)
                for b in range(B):
                    pe.wait_ge(a.q_sb, b + 1)
                    pe.wait_ge(a.k_sb, b + 1)
                    if l == 1 and b == 0:
                        pe.wait_ge(ff[0].y_rd, 4 * B)
                    for t in range(TT):
                        wait(pe, a.y_rd, 4 * (b - 1) + t + 1)
                        pe.matmul(roll[t][:, :], u["qT"][:, t * P:(t + 1) * P], u["kT"], start=True,
                                  stop=True).then_inc(a.s_mm, 1)
                    if b + 1 < B:
                        project_qk(l, b + 1)
                    else:
                        ffn_ahead(l, 0)
                    if l == 0 and b == 1:
                        pe.wait_ge(v_misc, 1)
                        pe.wait_ge(a.o_sb, b)
                        pe.matmul(misc_ps[:, 0:3], ones[:, :], asum3[:, :], start=True, stop=True).then_inc(t_misc, 1)
                    if l == 1 and b == 1:
                        pe.wait_ge(v_diag, 1)
                        pe.wait_ge(a.o_sb, b)
                        for t in range(2):
                            m = pe.matmul(misc_ps[:, t * P:(t + 1) * P], ones[:, :], diag3[:, t * P:(t + 1) * P],
                                          start=True, stop=True)
                        m.then_inc(t_misc, 1)
                    pe.wait_ge(a.exp, 4 * b + 4)
                    for kt in range(KT):
                        for t in range(TT):
                            m = pe.transpose(roll[kt][:, t * P:(t + 1) * P], u["pr"][:, t, kt * P:(kt + 1) * P],
                                             idf[:, :])
                        m.then_inc(a.t_mm, 1)
                    if b + 1 < B:
                        project_v(l, b + 1)
                    else:
                        ffn_ahead(l, 1)
                    wait(pe, a.o_sb, b)
                    if l == 0 and b == 1:
                        pe.wait_ge(v_misc, 2)
                    if l == 1 and b == 1:
                        pe.wait_ge(v_sc1, 1)
                    for kt in range(KT):
                        pe.wait_ge((a.pt_a, a.pt_d)[kt % 2], 2 * b + kt // 2 + 1)
                        m = pe.matmul(o_ps[:, :], u["v"][:, kt * D:(kt + 1) * D], u["pT"][:, kt, :],
                                      start=(kt == 0), stop=(kt == KT - 1))
                    m.then_inc(a.o_mm, 1)
                    if b >= 1:
                        pe.wait_ge(a.ln, b)
                        transpose_x(x_nat[:, (b - 1) * TT * H:b * TT * H], a.xt_mm, roll, range(KT))
                    elif l == 1:
                        pe.wait_ge(ff[0].xcp, 16 * B)
                        transpose_x(x_nat[:, (B - 1) * TT * H:B * TT * H], ff[0].xt_mm, roll, range(KT))
                    pe.wait_ge(a.o_sb, b + 1)
                    if l == 0 and b == 0:
                        pe.wait_ge(s_w0, 16)
                    for t in range(TT):
                        if l == 1 and b == 0:
                            pe.wait_ge(ff[0].xlo, 4 * (B - 1) + t + 1)
                        wait(pe, a.xlo, 4 * (b - 1) + t + 1)
                        pe.matmul(roll[t][:, :], u["oT"][:, t * P:(t + 1) * P], wo[:, :], start=True,
                                  stop=True).then_inc(a.y_mm, 1)
            def gate_up0(b, j, first, parts=(0, 1)):
                f, n, c0 = ff[0], b * NT0 + j, b * SEQ
                for k in parts:
                    ps, w, mm, used, tqs = ((g_ps[j % 2], tg, f.g_mm, f.silu, nf.tq_a),
                                            (u_ps[j % 2], tu, f.u_mm, f.h, nf.tq_d))[k]
                    if not first or j >= 2:
                        pe.wait_ge(used, n - 1)
                    if j in (SPLIT + 3, SPLIT + 4):
                        pe.wait_ge(tqs, 2 * (2 * b) + j - SPLIT - 2)
                    if j in (3, 4) and not first:
                        pe.wait_ge(tqs, 2 * (2 * b - 1) + j - 2)
                    if j in (7, 8) and not first:
                        pe.wait_ge(f.xlo, 4 * (b - 1) + 2 * (j - 7) + k + 1)
                    i = 0
                    for kt in range(KT):
                        for x in (xh, xl):
                            xv = x[:, kt, bass.ds(c0, SEQ)] if not first else x[:, kt, 0:SEQ]
                            m = pe.matmul(ps[:, :], w[:, kt, j * P:(j + 1) * P], xv,
                                          start=(i == 0), stop=(i == 2 * KT - 1))
                            i += 1
                    m.then_inc(mm, 1)

            def gate_up1(b, j, parts=(0, 1)):
                f, n, c0 = ff[1], b * NT1 + j, b * SEQ
                for part in parts:
                    ps, s0, mm, used = ((g_ps[j % 2], 0, f.g_mm, f.silu),
                                        (u_ps[j % 2], KT * NT1, f.u_mm, f.h))[part]
                    if ring_used(b, j):
                        pe.wait_ge(used, n - 1 if j else n)
                    i = 0
                    for kt in range(KT):
                        for w, x in ((w12h, xh), (w12h, xl), (w12l, xh)):
                            xv = x[:, kt, c0:c0 + SEQ] if isinstance(b, int) else x[:, kt, bass.ds(c0, SEQ)]
                            m = pe.matmul(ps[:, :], w[:, s0 + KT * j + kt, :], xv,
                                          start=(i == 0), stop=(i == 3 * KT - 1))
                            i += 1
                    m.then_inc(mm, 1)

            def ffn_ahead(l, j):
                if j == 0:
                    pe.wait_ge(at[l].xlo, 4)
                    if l == 0:
                        pe.wait_ge(v_tern, 8)
                    pe.wait_ge(at[l].q_sb, B)
                    pe.wait_ge(at[l].v_sb, B)
                    gate_up0(0, 0, True) if l == 0 else gate_up1(0, 0)
                else:
                    pe.wait_ge(at[l].k_sb, B)
                    gate_up0(0, 1, True, (0,)) if l == 0 else gate_up1(0, 1, (0,))

            def last_transpose_x(a, y_rd):
                pe.wait_ge(y_rd, 4 * B)
                pe.wait_ge(a.ln, B)
                transpose_x(x_nat[:, (B - 1) * TT * H:B * TT * H], a.xt_mm, roll, range(KT))

            def ffn0():
                f = ff[0]

                def down(n, j):
                    pe.wait_ge(f.lo, n + 1)
                    pe.ldweights(hring[:, j % 4, 0:P], tile_position=(0, 0))
                    pe.wait_ge(v_tern, 12)
                    for part, ring in enumerate((hring, lring)):
                        for t in range(TT):
                            m = pe.matmul(y_ps[t][:, :], ring[:, j % 4, t * P:(t + 1) * P], td[:, j, :],
                                          start=(j == 0 and part == 0), stop=(j == NT0 - 1 and part == 1))
                    m.then_inc(f.d_mm, 1)

                def tq(s, j, n):
                    e = (j + 1) % 2
                    pe.wait_ge(nf.lo, s + 1)
                    for i, (pb, src, s0, ns, used, d) in enumerate(
                            ((g_ps[e], nhi, 0, 8, f.silu, 0), (u_ps[e], nlo, 0, 8, f.h, 0),
                             (g_ps[1 - e], nhi, 8, 3, f.silu, 1), (u_ps[1 - e], nlo, 8, 3, f.h, 1))):
                        pe.wait_ge(used, n + d)
                        for k in range(ns):
                            m = pe.transpose(pb[:, :].bitcast(F16)[:, k * P:(k + 1) * P],
                                             src[:, (s0 + k) * P:(s0 + k + 1) * P], idh[:, :])
                        m.then_inc(f.tq_mm, 1)

                def body(b, first):
                    for j in range(NT0):
                        n = b * NT0 + j
                        if j == 0 and not first:
                            pe.wait_ge(at[0].xlo, 4 * (b + 1))
                        if not (first and j < 2):
                            gate_up0(b, j, first)
                        elif j == 1:
                            gate_up0(b, j, first, (1,))
                        if first and j == 3:
                            last_transpose_x(at[0], at[0].y_rd)
                        if first and j == 4:
                            pe.wait_ge(at[0].xlo, 4 * B)
                            down(0, 0)
                            down(1, 1)
                        if j >= 4 or not first:
                            if j == 2:
                                pe.wait_ge(f.y_rd, 4 * b)
                            down(n - 2, (j - 2) % NT0)
                        if j == 2 and not first:
                            tq(2 * b - 1, j, n)
                        if j == SPLIT + 2:
                            tq(2 * b, j, n)
                        if j == 6 and not first:
                            pe.wait_ge(f.ln, b)
                            for kt, (pb, used, d) in enumerate(((g_ps[1], f.silu, 0), (u_ps[1], f.h, 0),
                                                                (g_ps[0], f.silu, 1), (u_ps[0], f.h, 1))):
                                pe.wait_ge(used, n + d)
                                transpose_x(xs, f.xt_mm, {kt: pb}, [kt])
                body(0, True)
                with pe.Fori(1, B) as b:
                    body(b, False)
                for j in (NT0 - 2, NT0 - 1):
                    down((B - 1) * NT0 + j, j)
                tq(NSTR - 1, NT0 - 1, B * NT0 - 1)

            def ffn1():
                f = ff[1]

                def down_tile(b, t, j, c0, w):
                    rows = P if j < NT1 - 1 else LASTROWS
                    hi, lo = hidden1(b, j)
                    for part, (hp, wp) in enumerate(((hi, w3h), (hi, w3l), (lo, w3h))):
                        m = pe.matmul(y_ps[t][:, c0:c0 + w], hp[0:rows, t * P:(t + 1) * P], wp[0:rows, j, c0:c0 + w],
                                      start=(j == 0 and part == 0), stop=(j == NT1 - 1 and part == 2))
                    return m

                def transpose_w3(groups):
                    for i in groups:
                        t, r, s0, ns = tq3_groups[i]
                        if i % 4 == 0:
                            pe.wait_ge(n3.lop, 1)
                            pe.wait_ge(n3.lo, 2 * t + 1)
                        for part, (src, used) in enumerate(((n3h, n3.tq_a), (n3l, n3.tq_d))):
                            wait(pe, used, i - 1)
                            for k in range(ns):
                                c = r * F1 + (s0 + k) * P
                                m = pe.transpose(tq3_bank(i, part)[:, :].bitcast(F16)[:, k * P:(k + 1) * P],
                                                 src[:, c:c + P], idh[:, :])
                            m.then_inc(n3.tq_mm, 1)

                def down_all(b):
                    pe.wait_ge(f.y_rd, 4 * b)
                    for t in range(TT):
                        for j in range(NT1):
                            if t == 0:
                                pe.wait_ge(f.lo, b * NT1 + (j + 1))
                            m = down_tile(b, t, j, 0, H)
                        m.then_inc(f.d_mm, 1)

                gate_up1(0, 1, (1,))
                for j in range(2, NT1):
                    gate_up1(0, j)
                    if j == 3:
                        last_transpose_x(at[1], at[1].y_rd)
                    if j == 9:
                        pe.wait_ge(at[1].xlo, 4 * B)
                        transpose_w3((0, 1))
                pe.wait_ge(at[1].xlo, 8)
                gate_up1(1, 0)
                transpose_w3((2, 3))
                for j in range(1, AHEAD):
                    gate_up1(1, j)
                for half in range(2):
                    if half:
                        pe.wait_ge(f.silu, NT1 + AHEAD)
                        pe.wait_ge(f.h, NT1 + AHEAD)
                        transpose_w3(range(4, 8))
                    for used in (n3.tq_a, n3.tq_d):
                        pe.wait_ge(used, 4 * (half + 1))
                    for t in range(TT):
                        for j in range(NT1):
                            if half == 0 and t == 0:
                                pe.wait_ge(f.lo, j + 1)
                            m = down_tile(0, t, j, half * 2 * P, 2 * P)
                        if half:
                            m.then_inc(f.d_mm, 1)
                for j in range(AHEAD, NT1):
                    gate_up1(1, j)
                down_all(1)
                with pe.Fori(2, B) as b:
                    pe.wait_ge(at[1].xlo, 4 * (b + 1))
                    for j in range(NT1):
                        gate_up1(b, j)
                    down_all(b)

            pe.wait_ge(p_init, 4)
            attention(0)
            ffn0()
            pe.wait_ge(nf.tq_a, 2 * NSTR)
            pe.wait_ge(nf.tq_d, 2 * NSTR)
            pe.wait_ge(s_w1, 32)
            attention(1)
            ffn1()

        @block.vector
        def _(dve):
            TS, TTo, STT = dve.tensor_scalar, dve.tensor_tensor, dve.scalar_tensor_tensor

            def pow2_of(out, src):
                TS(out, src, TINY, None, ALU.max)
                dve.drain()
                o = out.bitcast(I32)
                TS(o, o, 0x7F800000, None, ALU.bitwise_and)
                dve.drain()

            def inverse_pow2(out, p2, bits):
                m = TS(out.bitcast(I32), p2.bitcast(I32), -1.0, float((254 + bits) << 23), ALU.mult, ALU.add)
                dve.drain()
                return m

            def tern(m, c):
                n = stream.index(("tern", m, c))
                chunk_wait(dve, n)
                i = 4 * m + c
                if i < BY_ACT:
                    dve.wait_ge(a_neg, i + 1)
                else:
                    TS(below[i % 2], raw[slot_of[n]], -1.0, thr[:, m, 0:1], ALU.mult, ALU.is_ge)
                    dve.drain()
                STT(out=tern_dst(m, c), in0=raw[slot_of[n]], scalar=thr[:, m, 0:1], in1=below[i % 2], op0=ALU.is_ge,
                    op1=ALU.subtract, **tern_mode(m)).then_inc(v_tern, 1)

            def absmax(m, c):
                n = stream.index(("amax", m, c))
                chunk_wait(dve, n)
                k0 = (4 * m + c) * SBLK
                dve.tensor_reduce(am[:, k0:k0 + SBLK], raw[slot_of[n]][:, 0:STRIPE].rearrange("p (b c) -> p b c", c=BLK),
                                  AX.X, ALU.max, apply_absolute_value=True).then_inc(v_raw, 1)

            def sums():
                dve.wait_ge(a_sum, 12)
                dve.tensor_reduce(asum3[:, :], asum[:, :].rearrange("p (m c) -> p m c", c=4), AX.X,
                                  ALU.add).then_inc(v_misc, 1)

            def thresholds():
                dve.wait_ge(t_misc, 1)
                TS(thr[:, :, 0], misc_ps[:, 0:3], 1.0 / (F0 * H), -float(np.float32(0.7)), ALU.mult, ALU.mult)
                dve.drain()
                TS(thr[:, :, 1], thr[:, :, 0], BIG, None, ALU.mult).then_inc(v_misc, 1)
                dve.drain()

            def ln_stats(src, tiles=range(TT)):
                for t in tiles:
                    dve.bn_stats(stats[:, t, :], src(t))
                dve.drain()
                for t in tiles:
                    dve.bn_aggr(mv[:, t, :], stats[:, t, :])
                dve.drain()

            def ln_rsqrt(c=slice(0, TT)):
                var, y, z = nv[:, 0, c], nv[:, 1, c], nv[:, 2, c]
                TS(var, mv[:, c, 1], EPS, None, ALU.add)
                dve.drain()
                TS(y.bitcast(I32), var.bitcast(I32), 1, None, ALU.logical_shift_right)
                dve.drain()
                TS(y.bitcast(I32), y.bitcast(I32), -1.0, float(0x5F3759DF), ALU.mult, ALU.add)
                dve.drain()
                for _ in range(3):
                    STT(out=z, in0=y, scalar=-0.5, in1=y, op0=ALU.mult, op1=ALU.mult)
                    dve.drain()
                    TTo(z, z, var, ALU.mult)
                    dve.drain()
                    STT(out=y, in0=z, scalar=1.5, in1=y, op0=ALU.add, op1=ALU.mult)
                    dve.drain()

            def ln_apply(src, dst, done, tiles=range(TT)):
                for t in tiles:
                    m = TS(dst(t), src(t), mv[:, t, 0:1], nv[:, 1, t:t + 1], ALU.subtract, ALU.mult)
                m.then_inc(done, 1)

            def layernorm(src, dst, done):
                ln_stats(src)
                ln_rsqrt()
                ln_apply(src, dst, done)

            def x_lo(a, kt, src, b):
                c = slice(b * SEQ, (b + 1) * SEQ) if isinstance(b, int) else bass.ds(b * SEQ, SEQ)
                STT(out=xl[:, kt, c], in0=src[:, :], scalar=XSCALE, in1=xh[:, kt, c], op0=ALU.mult,
                    op1=ALU.subtract).then_inc(a.xlo, 1)

            def attention(l):
                a, u = at[l], bufs[l]

                def k_evac(b):
                    dve.wait_ge(a.k_mm, b + 1)
                    if l == 0:
                        TS(u["kT"], k_ps[:, :], bcol[:, 0, 1:2], None, ALU.add).then_inc(a.k_sb, 1)
                    else:
                        TS(u["kT"], k_ps[:, :], fac[:, 6:7], bcol[:, 1, 1:2], ALU.mult, ALU.add).then_inc(a.k_sb, 1)

                def v_evac(b):
                    dve.wait_ge(a.v_mm, b + 1)
                    wait(dve, a.o_mm, b)
                    out = u["v"].rearrange("p (t f) -> p t f", t=TT)
                    src = v_ps[:, :].rearrange("p (t f) -> p t f", t=TT)
                    bias = bv_bc[:, l, :].unsqueeze(1).to_broadcast([P, TT, D])
                    if l == 0:
                        TTo(out, src, bias, ALU.add).then_inc(a.v_sb, 1)
                    else:
                        STT(out=out, in0=src, scalar=fac[:, 6:7], in1=bias, op0=ALU.mult,
                            op1=ALU.add).then_inc(a.v_sb, 1)

                def tile(b):
                    return lambda t: x_nat[:, (b * TT + t) * H:(b * TT + t + 1) * H]

                k_evac(0)
                v_evac(0)
                for b in range(B):
                    for t in range(TT):
                        dve.wait_ge(a.s_mm, 4 * b + t + 1)
                        dve.tensor_reduce(nmax[:, t:t + 1], roll[t][:, :], AX.X, ALU.max, negate=True).then_inc(a.mx, 1)
                    if l == 0 and b == 1:
                        sums()
                    if b >= 1:
                        layernorm(tile(b - 1), tile(b - 1), a.ln)
                    elif l == 1:
                        xs_tile = lambda t: xs[:, t * H:(t + 1) * H]
                        dve.wait_ge(ff[0].xb, B)
                        layernorm(xs_tile, xs_tile, ff[0].ln)
                    if b + 1 < B:
                        k_evac(b + 1)
                    if l == 0 and b == 1:
                        thresholds()
                    if l == 0 and b >= 1:
                        tern(b - 1, 0)
                    if l == 1 and b == 0:
                        w3_maxima(((1, 1), (0, 2)))
                    if l == 1 and b == 1:
                        scales_to_rows()
                    if l == 1:
                        steps_a(b, 0)
                    if l == 1 and b == 0:
                        dve.wait_ge(ff[0].xcp, 16 * B)
                    for kt in (1, 3):
                        dve.wait_ge(a.t_mm, 4 * b + kt + 1)
                        dve.tensor_copy(u["pT"][:, kt, :], roll[kt][:, :]).then_inc(a.pt_d, 1)
                    dve.wait_ge(a.exp, 4 * b + 4)
                    dve.reciprocal(rinv[:, :], rsum[:, :])
                    if l == 0 and b >= 1:
                        tern(b - 1, 1)
                    if l == 1:
                        steps_a(b, 1)
                    if b + 1 < B:
                        v_evac(b + 1)
                    if b >= 1:
                        for kt in range(KT):
                            dve.wait_ge(a.xhi, 4 * (b - 1) + kt + 1)
                            x_lo(a, kt, roll[kt], b - 1)
                    elif l == 1:
                        last_x_lo(ff[0])
                        w3_maxima(((1, 3), (0, 0)))
                    if l == 1:
                        steps_a(b, 2)
                    dve.drain()
                    for t in range(TT):
                        dve.wait_ge(a.y_mm, 4 * b + t + 1)
                        dve.wait_ge(a.xb, 4 * b + t + 1)
                        STT(out=tile(b)(t), in0=roll[t][:, :], scalar=rinv[:, t:t + 1], in1=tile(b)(t), op0=ALU.mult,
                            op1=ALU.add).then_inc(a.y_rd, 1)
                    if l == 1 and b == 0:
                        w3_scales()
                        w3_diag()
                    if l == 0 and b in (1, 2):
                        tern(b - 1, 2)
                        tern(b - 1, 3)
                        for m, c in (((0, 0), (0, 1)), ((0, 2), (0, 3), (1, 0)))[b - 1]:
                            absmax(m, c)
                    dve.drain()
            def last_layernorm(l):
                def tile(t):
                    return x_nat[:, ((B - 1) * TT + t) * H:((B - 1) * TT + t + 1) * H]
                layernorm(tile, tile, at[l].ln)

            def last_x_lo(a):
                for kt in range(KT):
                    dve.wait_ge(a.xhi, 4 * (B - 1) + kt + 1)
                    x_lo(a, kt, roll[kt], B - 1)

            def stt(ph, k, w, slot, m):
                dve.wait_ge(ph.rel, m + 1)
                if k == 0:
                    TS(nacc[:, 0:w], nrel[slot][:, 0:w], float(STEPS[0]), float(NF4[0]), ALU.min,
                       ALU.add).then_inc(ph.stt, 1)
                else:
                    STT(out=nacc[:, 0:w], in0=nrel[slot][:, 0:w], scalar=float(STEPS[k]), in1=nacc[:, 0:w],
                        op0=ALU.min, op1=ALU.add).then_inc(ph.stt, 1)
                dve.drain()

            def dequant(ph, scales, nb):
                v = nacc[:, 0:nb * BLK].rearrange("p (b c) -> p b c", c=BLK)
                TTo(v, v, scales.unsqueeze(2).to_broadcast([P, nb, BLK]), ALU.mult).then_inc(ph.dq, 1)

            def ffn0():
                f = ff[0]

                def nf_lo(s):
                    dve.wait_ge(nf.hi, s + 1)
                    TTo(nlo, nacc, nhi, ALU.subtract).then_inc(nf.lo, 1)
                    dve.drain()

                def tq_lo(s, j):
                    e = (j + 1) % 2
                    for i, (pb, s0, ns) in enumerate(((u_ps[e], 0, 8), (u_ps[1 - e], 8, 3))):
                        dve.wait_ge(f.tq_mm, 4 * s + (2, 4)[i])
                        dve.tensor_copy(w12l[:, bass.ds(s * NT1 + s0, ns), :],
                                        pb[:, :].bitcast(F16)[:, 0:ns * P].rearrange("p (s f) -> p s f", f=P)
                                        ).then_inc(nf.tq_d, 1)

                def tile_of(t):
                    return xs[:, t * H:(t + 1) * H]

                def scale_y(b):
                    dve.wait_ge(f.d_mm, NT0 * (b + 1))
                    for t in range(TT):
                        TTo(tile_of(t), y_ps[t][:, :], sc_bc[:, :], ALU.mult).then_inc(f.y_rd, 1)

                def body(b, first):
                    for j in range(NT0):
                        n = b * NT0 + j
                        half = int(j >= SPLIT)
                        s = 2 * b + half
                        dve.wait_ge(f.u_mm, n + 1)
                        dve.wait_ge(f.silu, n + 1)
                        STT(out=sring[:, j % 2, :], in0=u_ps[j % 2][:, :], scalar=u_sc[:, j:j + 1],
                            in1=sring[:, j % 2, :], op0=ALU.mult, op1=ALU.mult).then_inc(f.h, 1)
                        if j == SPLIT or (j == 0 and not first):
                            nf_lo(s - 1)
                        if not first:
                            if j == 1:
                                scale_y(b - 1)
                            if j == 3:
                                dve.wait_ge(f.xb, b)
                                ln_stats(tile_of)
                            if j == 4:
                                ln_rsqrt()
                            if j == 5:
                                ln_apply(tile_of, tile_of, f.ln)
                        elif j == 1:
                            last_layernorm(0)
                        elif j == 2:
                            last_x_lo(at[0])
                            tern(2, 2)
                            tern(2, 3)
                        elif j == 3:
                            for c in range(1, 4):
                                absmax(1, c)
                            dve.drain()
                            w12_scales()
                        elif j == 4:
                            dve.wait_ge(s_wraw1, 16)
                            dve.tensor_reduce(fac[:, 4:5], wraw1, AX.X, ALU.max,
                                              apply_absolute_value=True).then_inc(v_wmax, 1)
                        elif j == 10:
                            split_wqkv1()
                        share = SHARE_0 if first and half == 0 else SHARE[half]
                        k0 = sum(share[:j])
                        for k in range(k0, k0 + share[j]):
                            stt(nf, k, STRIPE, (k + half) % 2, s * NB + k)
                        if j == 9 and not first:
                            dve.wait_ge(f.xcp, b * 16)
                            dve.wait_ge(f.xt_mm, 4 * b)
                        if j in (SPLIT - 1, NT0 - 1):
                            cols = am[:, bass.ds(s * SBLK, SBLK)]
                            dequant(nf, cols, SBLK)
                        if j == 2 and not first:
                            tq_lo(2 * b - 1, j)
                        if j == SPLIT + 2:
                            tq_lo(2 * b, j)
                        if j == 6 and not first:
                            for kt, pb in enumerate((g_ps[1], u_ps[1], g_ps[0], u_ps[0])):
                                dve.wait_ge(f.xhi, 4 * (b - 1) + kt + 1)
                                x_lo(f, kt, pb, b - 1)
                body(0, True)
                with dve.Fori(1, B) as b:
                    body(b, False)
                nf_lo(NSTR - 1)
                scale_y(B - 1)
                tq_lo(NSTR - 1, NT0 - 1)

            def steps_w3(c, k0, n):
                w = w3_part[c][3] * BLK
                for k in range(k0, k0 + n):
                    stt(n3, k, w, (c * NB + k) % 2, c * NB + k)

            def steps_a(b, i):
                k0 = sum(sum(p) for p in SHARE_A[:b]) + sum(SHARE_A[b][:i])
                steps_w3(0, k0, SHARE_A[b][i])

            def w3_dequant(c):
                t, _, b0, nb = w3_part[c]
                k0 = 8 * SBLK + t * PBLK + b0
                dequant(n3, am[:, k0:k0 + nb], nb)

            def w3_lo(c):
                _, half, _, nb = w3_part[c]
                w, cs = nb * BLK, half * STRIPE
                dve.wait_ge(n3.hi, c + 1)
                TTo(n3l[:, cs:cs + w], nacc[:, 0:w], n3h[:, cs:cs + w], ALU.subtract).then_inc(n3.lo, 1)
                dve.drain()

            def w3_tq_lo(i):
                t, r, s0, ns = tq3_groups[i]
                dve.wait_ge(n3.tq_mm, 2 * i + 2)
                dve.tensor_copy(w3l[:, s0:s0 + ns, (2 * t + r) * P:(2 * t + r + 1) * P],
                                tq3_bank(i, 1)[:, :].bitcast(F16)[:, 0:ns * P].rearrange(
                                    "p (s f) -> p s f", f=P)).then_inc(n3.tq_d, 1)

            def ffn1():
                f = ff[1]

                def out_view(v):
                    return v.rearrange("q (t p r) -> q t r p", t=2, r=2)

                def finish(b, t):
                    o = b * (TT * H) + t * H
                    x = x_nat[:, o:o + H] if isinstance(o, int) else x_nat[:, bass.ds(o, H)]
                    tmp = ytmp[:, t * H:(t + 1) * H]
                    dve.wait_ge(f.d_mm, b * TT + (t + 1))
                    TTo(tmp, y_ps[t][:, :], sc_bc[:, :], ALU.mult).then_inc(f.y_rd, 1)
                    dve.drain()
                    TTo(out_view(x), tmp.rearrange("q (t r p) -> q t r p", t=2, r=2), out_view(x), ALU.add)
                    dve.drain()
                    ln_stats(lambda _: x, (t,))
                    ln_rsqrt(slice(t, t + 1))
                    ln_apply(lambda _: x, lambda _: x, f.ln, (t,))

                def silu_up(b, j):
                    n = b * NT1 + j
                    dve.wait_ge(f.u_mm, n + 1)
                    dve.wait_ge(f.silu, n + 1)
                    STT(out=sring[:, j % 2, :], in0=u_ps[j % 2][:, :], scalar=u1_sc[:, j:j + 1],
                        in1=sring[:, j % 2, :], op0=ALU.mult, op1=ALU.mult).then_inc(f.h, 1)

                for j in range(NT1):
                    silu_up(0, j)
                    if j == 1:
                        last_layernorm(1)
                    if j == 1:
                        dve.wait_ge(n3.lop, 1)
                    if j == 7:
                        w3_lo(1)
                    for c in (1, 2):
                        steps_w3(c, sum(SHARE_F[c - 1][:j]), SHARE_F[c - 1][j])
                    if j == 2:
                        last_x_lo(at[1])
                    if j == 6:
                        w3_dequant(1)
                w3_tq_lo(0)
                w3_tq_lo(1)
                k0 = sum(SHARE_F[1])
                for j in range(AHEAD):
                    silu_up(1, j)
                    if j == 0:
                        w3_tq_lo(2)
                        w3_tq_lo(3)
                        steps_w3(2, k0, NB - k0 - 2)
                    if j == 1:
                        steps_w3(2, NB - 2, 2)
                        w3_dequant(2)
                    if j == 2:
                        w3_lo(2)
                        steps_w3(3, 0, 2)
                steps_w3(3, 2, NB - 2)
                w3_dequant(3)
                w3_lo(3)
                for i in range(4, 8):
                    w3_tq_lo(i)
                for j in range(AHEAD, NT1):
                    silu_up(1, j)
                    if j < AHEAD + TT:
                        finish(0, j - AHEAD)
                for t in range(TT):
                    finish(1, t)
                with dve.Fori(2, B) as b:
                    for j in range(NT1):
                        silu_up(b, j)
                    for t in range(TT):
                        finish(b, t)

            def split_wqkv1():
                dve.wait_ge(p_red, 2)
                pow2_of(fac[:, 6:7], fac[:, 5:6])
                inverse_pow2(fac[:, 7:8], fac[:, 6:7], WBITS)
                dve.wait_ge(at[0].v_mm, B)
                TS(wraw1, wraw1, fac[:, 7:8], None, ALU.mult)
                dve.drain()
                dve.tensor_copy(wq_h, wraw1)
                dve.drain()
                TTo(wq_l, wraw1, wq_h, ALU.subtract)
                TS(fac[:, 6:7], fac[:, 6:7], 2.0 ** -(WBITS + XS_BITS), None, ALU.mult)
                dve.drain()
                TS(fac[:, 7:8], fac[:, 6:7], SCALE, None, ALU.mult)

            def block_scales(c0, nr, nb, r0):
                v, n = am[:, c0:c0 + nr * nb], nr * nb
                TS(rc[:, c0:c0 + n], v, 1e-38, None, ALU.max)
                v = v.rearrange("p (r b) -> p r b", b=nb)
                dve.tensor_reduce(tmp16[:, r0:r0 + nr], v, AX.X, ALU.max)
                dve.drain()
                dve.reciprocal(rc[:, c0:c0 + n], rc[:, c0:c0 + n])
                pow2_of(rp2[:, r0:r0 + nr], tmp16[:, r0:r0 + nr])
                inverse_pow2(rinvp2[:, r0:r0 + nr], rp2[:, r0:r0 + nr], WBITS)
                TTo(v, v, rinvp2[:, r0:r0 + nr].unsqueeze(2).to_broadcast([P, nr, nb]), ALU.mult).then_inc(v_rc, 1)
                dve.drain()

            def w12_scales():
                block_scales(0, 2 * NT1, 8, 0)
                TTo(tmp16[:, 0:NT1], rp2[:, 0:NT1], rp2[:, NT1:2 * NT1], ALU.mult)
                dve.drain()
                dve.tensor_reduce(fac[:, 8:9], tmp16[:, 0:NT1], AX.X, ALU.max).then_inc(v_init, 1)
                dve.drain()

            def w3_maxima(stripes):
                for slot, c in stripes:
                    t, _, b0, nb = w3_part[c]
                    dve.wait_ge(s_am3[slot], 16 * (1 if c in (1, 2) else 2))
                    k0 = 8 * SBLK + t * PBLK + b0
                    dve.tensor_reduce(am[:, k0:k0 + nb], am3[slot][:, 0:nb * BLK].rearrange("p (b c) -> p b c", c=BLK),
                                      AX.X, ALU.max, apply_absolute_value=True).then_inc(v_am3, 1)

            def w3_scales():
                dve.drain()
                block_scales(8 * SBLK, 2, PBLK, 2 * NT1)
                dve.wait_ge(p_red, 3)
                TS(fac[:, 10:11], fac[:, 9:10], TINY, None, ALU.max)
                dve.drain()
                inverse_pow2(fac[:, 11:12], fac[:, 10:11], -5)
                TS(g1_sc[:, :], rp2[:, 0:NT1], 2.0 ** -(WBITS + XS_BITS), None, ALU.mult)
                TS(u1_sc[:, :], rp2[:, NT1:2 * NT1], 2.0 ** -(WBITS + XS_BITS), fac[:, 11:12], ALU.mult, ALU.mult)
                TS(rp2[:, 22:24], rp2[:, 22:24], fac[:, 10:11], 2.0 ** (5 - WBITS), ALU.mult, ALU.mult)
                dve.drain()

            def w3_diag():
                for t in range(2):
                    m = TS(diag3[:, t * P:(t + 1) * P], idf[:, :], rp2[:, 22 + t:23 + t], None, ALU.mult)
                m.then_inc(v_diag, 1)

            def scales_to_rows():
                dve.wait_ge(t_misc, 2)
                src = misc_ps[:, 0:2 * P].rearrange("p (t f) -> p t f", t=2)
                dst = sc_bc[:, :].rearrange("p (t r f) -> p t r f", t=2, r=2)
                for r in range(2):
                    m = dve.tensor_copy(dst[:, :, r, :], src)
                m.then_inc(v_sc1, 1)

            dve.memset(asum3[:, :], 0.0)
            dve.wait_ge(s_const, 16 * 7)
            TTo(tmp16[:, 0:NT0], g_sc[:, :], u_sc[:, :], ALU.mult)
            dve.drain()
            dve.tensor_reduce(fac[:, 0:1], tmp16[:, 0:NT0], AX.X, ALU.max, apply_absolute_value=True
                              ).then_inc(v_init, 1)
            TS(bqs[:, 0:2], bcol[:, :, 0], SCALE, None, ALU.mult).then_inc(v_init, 1)
            dve.wait_ge(p_red, 1)
            pow2_of(fac[:, 2:3], fac[:, 1:2])
            inverse_pow2(fac[:, 3:4], fac[:, 2:3], -4)
            TS(g_sc[:, :], g_sc[:, :], 1.0 / XSCALE, None, ALU.mult)
            TS(u_sc[:, :], u_sc[:, :], 1.0 / XSCALE, fac[:, 3:4], ALU.mult, ALU.mult)
            TS(sc_bc[:, :], sc_bc[:, :], fac[:, 2:3], 2.0 ** 4, ALU.mult, ALU.mult).then_inc(v_init, 1)
            dve.drain()
            attention(0)
            ffn0()
            dve.memset(n3h[:, PAIR:NATW], 0.0)
            dve.memset(n3l[:, PAIR:NATW], 0.0)
            dve.drain()
            attention(1)
            ffn1()

    return nc


def kernel(**inputs):
    import numpy as _np
    import concourse.bacc as _bacc
    from concourse import mybir as _mybir
    from concourse.bass_utils import run_bass_kernel_spmd as _run

    inp = {k: _np.asarray(v) for k, v in inputs.items()}
    c = _np.ascontiguousarray
    x = inp["L0_attn_x"].reshape(B * SEQ, H)
    pad = ((0, NT1 * P - F1), (0, 0))

    def nat_tiles(w):
        t = _np.pad(w, pad).reshape(NT1, P, H).transpose(1, 0, 2).reshape(P, 4, STRIPE)
        return t.transpose(1, 0, 2)

    arrays = {
        "x_nat_in": c(x.reshape(B, TT, P, H).transpose(0, 2, 1, 3)),
        "x_T_in": c(x.reshape(B, SEQ, KT, P).transpose(0, 3, 2, 1)),
        "wqkv0_in": c(inp["L0_attn_Wqkv"].reshape(KT, P, 3 * D).transpose(1, 0, 2)),
        "wqkv1_in": c(inp["L1_attn_Wqkv"].reshape(KT, P, 3 * D).transpose(1, 0, 2).reshape(P, -1)),
        "bcol_in": c(_np.stack([inp["L0_attn_bqkv"].reshape(3, D).T, inp["L1_attn_bqkv"].reshape(3, D).T], 1)),
        "bv_in": c(_np.stack([inp["L0_attn_bqkv"][2 * D:], inp["L1_attn_bqkv"][2 * D:]])),
        "bo_in": c(_np.stack([inp["L0_attn_bo"], inp["L1_attn_bo"]])),
        "wo_in": c(_np.stack([inp["L0_attn_Wo"], inp["L1_attn_Wo"]])),
        "gsc_in": c(inp["L0_ffn_gate_scale"].reshape(NT0, P).T),
        "usc_in": c(inp["L0_ffn_up_scale"].reshape(NT0, P).T),
        "dsc_in": c(inp["L0_ffn_down_scale"].reshape(1, H)),
        "gate_T_in": c(inp["L0_ffn_gate_w"].T.reshape(KT, P, F0)),
        "up_T_in": c(inp["L0_ffn_up_w"].T.reshape(KT, P, F0)),
        "down_T_in": c(inp["L0_ffn_down_w"].T.reshape(KT, KT, P, H).transpose(0, 2, 1, 3)),
        "w12_in": c(_np.concatenate([nat_tiles(inp["L1_ffn_w1"]), nat_tiles(inp["L1_ffn_w2"])])),
        "w3_in": c(inp["L1_ffn_w3"].reshape(2, P, PAIR)),
    }
    nc = _bacc.Bacc("TRN2", target_bir_lowering=False, num_devices=1)
    ap = {n: nc.dram_tensor(n, a.shape, _mybir.dt.from_np(a.dtype), kind="ExternalInput").ap()
          for n, a in arrays.items()}
    out = nc.dram_tensor("out", (B, P, TT, H), F32, kind="ExternalOutput").ap()

    def rows(v):
        return v.unsqueeze(0).to_broadcast([P, v.shape[0]])

    io = {
        "xn": [ap["x_nat_in"][b] for b in range(B)], "xT": [ap["x_T_in"][b] for b in range(B)],
        "wqkv": [ap["wqkv0_in"]], "wqkv1": ap["wqkv1_in"], "bcol": ap["bcol_in"],
        "bv": [rows(ap["bv_in"][l]) for l in range(2)], "bo": [rows(ap["bo_in"][l]) for l in range(2)],
        "wo": [ap["wo_in"][l] for l in range(2)], "gsc": ap["gsc_in"], "usc": ap["usc_in"],
        "dsc": rows(ap["dsc_in"][0]),
        "tern": [[ap["gate_T_in"][k] for k in range(KT)], [ap["up_T_in"][k] for k in range(KT)],
                 [ap["down_T_in"][k] for k in range(KT)]],
        "w12n": ap["w12_in"], "w3n": [ap["w3_in"][t] for t in range(2)], "out": out,
    }
    build(nc, io)
    r = _run(nc, [arrays], core_ids=[0])
    got = r.results[0]["out"]
    return c(got.transpose(0, 2, 1, 3)).reshape(B, SEQ, H)
```
